# Optimizing a Trainium2 kernel written in Bass

```python
import numpy as np
import jax
import jax.numpy as jnp

def _softmax(x, axis=-1):
    return jax.nn.softmax(x, axis=axis)

def _gelu(x):
    return jax.nn.gelu(x, approximate=True)

def _silu(x):
    return jax.nn.silu(x)

def _sigmoid(x):
    return jax.nn.sigmoid(x)

def _layernorm(x, axis=-1, eps=1e-05):
    m = jnp.mean(x, axis=axis, keepdims=True)
    v = jnp.var(x, axis=axis, keepdims=True)
    return (x - m) / jnp.sqrt(v + eps)

def _scatter_add(tgt, idx, src, axis=0):
    return tgt.at[idx].add(src)

def _segment_sum(src, seg, n):
    return jax.ops.segment_sum(src, seg, n)
kernel_name = 'mk_perceiver_d1_seqx_r8_1e314c'

def setup_inputs(seed: int=0):
    np.random.seed(seed)
    _w = jnp.asarray

    def _rec_inputs():
        import jax
        import jax.numpy as jnp
        _rk = jax.random.key(seed)
        x = 7.22e-05 + 1 * jax.random.normal(jax.random.fold_in(_rk, 1), (1, 128, 512), jnp.float32)
        _lenS = 128 - jax.random.randint(jax.random.fold_in(_rk, 7), (1,), 0, max(1, 128 // 4) + 1, jnp.int32)
        _lenS2 = 2048 - jax.random.randint(jax.random.fold_in(_rk, 8), (1,), 0, max(1, 2048 // 4) + 1, jnp.int32)
        _ctx_4096P = jax.random.normal(jax.random.fold_in(_rk, 11), (1, 16, 512), jnp.float32)
        _ctx_4096c = jax.random.dirichlet(jax.random.fold_in(_rk, 511), 0.3 * jnp.ones((16,), jnp.float32), (1, 2048))
        _ctx_4096t = jnp.einsum('bsk,bkd->bsd', _ctx_4096c, _ctx_4096P)
        _ctx_4096t = _ctx_4096t * jax.lax.rsqrt(jnp.mean(jnp.square(_ctx_4096t)) + 1e-12) * 0.953939
        ctx_4096 = 4.13588e-05 + 0.999923 * (_ctx_4096t + 0.3 * jax.random.normal(jax.random.fold_in(_rk, 611), (1, 2048, 512), jnp.float32))
        return (x, ctx_4096)
    x, ctx_4096 = _rec_inputs()

    def _L0_xattn_setup():
        import jax, jax.numpy as jnp
        import numpy as np
        DIM = 512
        NUM_HEADS = 32
        NUM_KV_HEADS = 8
        HEAD_DIM = DIM // NUM_HEADS
        KV_DIM = DIM // (NUM_HEADS // NUM_KV_HEADS)
        B, S = (1, 256)
        key = jax.random.key(seed)
        ks = jax.random.split(key, 7)
        w_scale = DIM ** (-0.5)
        return {'query': jax.random.normal(ks[0], (B, S, DIM), jnp.float32), 'key': jax.random.normal(ks[1], (B, S, DIM), jnp.float32), 'value': jax.random.normal(ks[2], (B, S, DIM), jnp.float32), 'Wq': jax.random.normal(ks[3], (DIM, DIM), jnp.float32) * w_scale, 'Wk': jax.random.normal(ks[4], (DIM, KV_DIM), jnp.float32) * w_scale, 'Wv': jax.random.normal(ks[5], (DIM, KV_DIM), jnp.float32) * w_scale, 'Wo': jax.random.normal(ks[6], (DIM, DIM), jnp.float32) * w_scale}
    _L0_xattn_all = _L0_xattn_setup()
    _L0_xattn_in = {k: v for k, v in _L0_xattn_all.items() if k in ('Wq', 'Wk', 'Wv', 'Wo')}
    del _L0_xattn_all

    def _L0_attn_setup():
        import jax, jax.numpy as jnp
        import numpy as np
        H_SIZE = 512
        NH = 128
        HD = 64
        SS = 128
        K = 4
        NG = 8
        CHUNK = 128
        INTER = NH * HD
        CONV_DIM = INTER + 2 * NG * SS
        PROJ = INTER + CONV_DIM + NH
        DT_MIN, DT_MAX = (0.001, 100.0)
        EPS = 1e-05
        GROUP = INTER // NG

        def _ssd(x, Bm, Cm, D, dt, dt_bias):
            Bsz, S, H, P = x.shape
            N = Bm.shape[-1]
            A = -jnp.arange(1, H + 1, dtype=jnp.float32)
            dt = jnp.clip(jax.nn.softplus(dt + dt_bias), DT_MIN, DT_MAX)
            rep = H // Bm.shape[2]
            Bh = jnp.repeat(Bm, rep, axis=2)
            Ch = jnp.repeat(Cm, rep, axis=2)
            nc, L = (S // CHUNK, CHUNK)
            xc = x.reshape(Bsz, nc, L, H, P)
            dtc = dt.reshape(Bsz, nc, L, H)
            Bc = Bh.reshape(Bsz, nc, L, H, N)
            Cc = Ch.reshape(Bsz, nc, L, H, N)
            dA = jnp.swapaxes(dtc, 2, 3) * A[None, None, :, None]
            cs = jnp.cumsum(dA, axis=-1)
            seg = cs[..., :, None] - cs[..., None, :]
            tri = jnp.tril(jnp.ones((L, L), dtype=bool))
            Lmat = jnp.where(tri, jnp.exp(seg), 0.0)
            xdt = xc * dtc[..., None]
            scores = jnp.einsum('bclhn,bcshn->bchls', Cc, Bc) * Lmat
            Ydiag = jnp.einsum('bchls,bcshp->bclhp', scores, xdt)
            decay_states = jnp.exp(cs[..., -1:] - cs)
            states = jnp.einsum('bclhn,bchl,bclhp->bchpn', Bc, decay_states, xdt)
            chunk_decay = jnp.exp(cs[..., -1])

            def step(carry, inp):
                st, cd = inp
                new = carry * cd[:, :, None, None] + st
                return (new, carry)
            st_seq = jnp.moveaxis(states, 1, 0)
            cd_seq = jnp.moveaxis(chunk_decay, 1, 0)
            init = jnp.zeros_like(st_seq[0])
            _, prev = jax.lax.scan(step, init, (st_seq, cd_seq))
            prev = jnp.moveaxis(prev, 0, 1)
            Yoff = jnp.einsum('bclhn,bchpn,bchl->bclhp', Cc, prev, jnp.exp(cs))
            Y = (Ydiag + Yoff).reshape(Bsz, S, H, P) + x * D[None, None, :, None]
            return Y
        key = jax.random.key(seed)
        ks = jax.random.split(key, 5)
        s = 0.02
        return {'hidden_states': jax.random.normal(ks[0], (1, 256, H_SIZE), jnp.float32), 'in_proj_w': jax.random.normal(ks[1], (PROJ, H_SIZE), jnp.float32) * s, 'conv_w': jax.random.normal(ks[2], (CONV_DIM, 1, K), jnp.float32) * 0.1, 'conv_b': jnp.zeros((CONV_DIM,), jnp.float32), 'dt_bias': jnp.ones((NH,), jnp.float32), 'D': jnp.ones((NH,), jnp.float32), 'norm_w': jnp.ones((INTER,), jnp.float32), 'out_proj_w': jax.random.normal(ks[3], (H_SIZE, INTER), jnp.float32) * s}
    _L0_attn_all = _L0_attn_setup()
    _L0_attn_in = {k: v for k, v in _L0_attn_all.items() if k in ('in_proj_w', 'conv_w', 'conv_b', 'dt_bias', 'D', 'norm_w', 'out_proj_w')}
    del _L0_attn_all

    def _L0_ffn_setup():
        import jax, jax.numpy as jnp
        import numpy as np
        TOP_K = 2
        key = jax.random.key(seed)
        k0, k1, k2 = jax.random.split(key, 3)
        B, S, D, H, E = (4, 256, 512, 512, 8)
        sc = 1.0 / np.sqrt(D).astype(np.float32)
        x = jax.random.normal(k0, (B, S, D), dtype=jnp.float32)
        W_gate = jax.random.normal(k1, (D, E), dtype=jnp.float32) * sc
        b_gate = jnp.zeros((E,), dtype=jnp.float32)
        W_e = jax.random.normal(k2, (E, D, H), dtype=jnp.float32) * sc
        b_e = jnp.zeros((E, H), dtype=jnp.float32)
        return {'x': x, 'W_gate': W_gate, 'b_gate': b_gate, 'W_e': W_e, 'b_e': b_e}
    _L0_ffn_all = _L0_ffn_setup()
    _L0_ffn_in = {k: v for k, v in _L0_ffn_all.items() if k in ('W_gate', 'b_gate', 'W_e', 'b_e')}
    del _L0_ffn_all
    return {'x': x, 'ctx_4096': ctx_4096, 'L0_xattn_Wq': _L0_xattn_in['Wq'], 'L0_xattn_Wk': _L0_xattn_in['Wk'], 'L0_xattn_Wv': _L0_xattn_in['Wv'], 'L0_xattn_Wo': _L0_xattn_in['Wo'], 'L0_attn_in_proj_w': _L0_attn_in['in_proj_w'], 'L0_attn_conv_w': _L0_attn_in['conv_w'], 'L0_attn_conv_b': _L0_attn_in['conv_b'], 'L0_attn_dt_bias': _L0_attn_in['dt_bias'], 'L0_attn_D': _L0_attn_in['D'], 'L0_attn_norm_w': _L0_attn_in['norm_w'], 'L0_attn_out_proj_w': _L0_attn_in['out_proj_w'], 'L0_ffn_W_gate': _L0_ffn_in['W_gate'], 'L0_ffn_b_gate': _L0_ffn_in['b_gate'], 'L0_ffn_W_e': _L0_ffn_in['W_e'], 'L0_ffn_b_e': _L0_ffn_in['b_e']}

def reference(x, ctx_4096, L0_xattn_Wq, L0_xattn_Wk, L0_xattn_Wv, L0_xattn_Wo, L0_attn_in_proj_w, L0_attn_conv_w, L0_attn_conv_b, L0_attn_dt_bias, L0_attn_D, L0_attn_norm_w, L0_attn_out_proj_w, L0_ffn_W_gate, L0_ffn_b_gate, L0_ffn_W_e, L0_ffn_b_e):
    import jax
    import jax.numpy as jnp

    def _L0_xattn_ref(query, key, value, Wq, Wk, Wv, Wo):
        import jax, jax.numpy as jnp
        import numpy as np
        DIM = 512
        NUM_HEADS = 32
        NUM_KV_HEADS = 8
        HEAD_DIM = DIM // NUM_HEADS
        KV_DIM = DIM // (NUM_HEADS // NUM_KV_HEADS)
        B, S = (1, 256)
        b, sq, _ = query.shape
        _, sk, _ = key.shape
        rep = NUM_HEADS // NUM_KV_HEADS
        q = (query @ Wq).reshape(b, sq, NUM_HEADS, HEAD_DIM).transpose(0, 2, 1, 3)
        k = (key @ Wk).reshape(b, sk, NUM_KV_HEADS, HEAD_DIM).transpose(0, 2, 1, 3)
        v = (value @ Wv).reshape(b, sk, NUM_KV_HEADS, HEAD_DIM).transpose(0, 2, 1, 3)
        k = jnp.repeat(k, rep, axis=1)
        v = jnp.repeat(v, rep, axis=1)
        scale = HEAD_DIM ** (-0.5)
        scores = jnp.einsum('bhqd,bhkd->bhqk', q, k) * scale
        probs = jax.nn.softmax(scores, axis=-1)
        out = jnp.einsum('bhqk,bhkd->bhqd', probs, v)
        out = out.transpose(0, 2, 1, 3).reshape(b, sq, DIM)
        return out @ Wo

    def _L0_attn_ref(hidden_states, in_proj_w, conv_w, conv_b, dt_bias, D, norm_w, out_proj_w):
        import jax, jax.numpy as jnp
        import numpy as np
        H_SIZE = 512
        NH = 128
        HD = 64
        SS = 128
        K = 4
        NG = 8
        CHUNK = 128
        INTER = NH * HD
        CONV_DIM = INTER + 2 * NG * SS
        PROJ = INTER + CONV_DIM + NH
        DT_MIN, DT_MAX = (0.001, 100.0)
        EPS = 1e-05
        GROUP = INTER // NG

        def _ssd(x, Bm, Cm, D, dt, dt_bias):
            Bsz, S, H, P = x.shape
            N = Bm.shape[-1]
            A = -jnp.arange(1, H + 1, dtype=jnp.float32)
            dt = jnp.clip(jax.nn.softplus(dt + dt_bias), DT_MIN, DT_MAX)
            rep = H // Bm.shape[2]
            Bh = jnp.repeat(Bm, rep, axis=2)
            Ch = jnp.repeat(Cm, rep, axis=2)
            nc, L = (S // CHUNK, CHUNK)
            xc = x.reshape(Bsz, nc, L, H, P)
            dtc = dt.reshape(Bsz, nc, L, H)
            Bc = Bh.reshape(Bsz, nc, L, H, N)
            Cc = Ch.reshape(Bsz, nc, L, H, N)
            dA = jnp.swapaxes(dtc, 2, 3) * A[None, None, :, None]
            cs = jnp.cumsum(dA, axis=-1)
            seg = cs[..., :, None] - cs[..., None, :]
            tri = jnp.tril(jnp.ones((L, L), dtype=bool))
            Lmat = jnp.where(tri, jnp.exp(seg), 0.0)
            xdt = xc * dtc[..., None]
            scores = jnp.einsum('bclhn,bcshn->bchls', Cc, Bc) * Lmat
            Ydiag = jnp.einsum('bchls,bcshp->bclhp', scores, xdt)
            decay_states = jnp.exp(cs[..., -1:] - cs)
            states = jnp.einsum('bclhn,bchl,bclhp->bchpn', Bc, decay_states, xdt)
            chunk_decay = jnp.exp(cs[..., -1])

            def step(carry, inp):
                st, cd = inp
                new = carry * cd[:, :, None, None] + st
                return (new, carry)
            st_seq = jnp.moveaxis(states, 1, 0)
            cd_seq = jnp.moveaxis(chunk_decay, 1, 0)
            init = jnp.zeros_like(st_seq[0])
            _, prev = jax.lax.scan(step, init, (st_seq, cd_seq))
            prev = jnp.moveaxis(prev, 0, 1)
            Yoff = jnp.einsum('bclhn,bchpn,bchl->bclhp', Cc, prev, jnp.exp(cs))
            Y = (Ydiag + Yoff).reshape(Bsz, S, H, P) + x * D[None, None, :, None]
            return Y
        Bsz, S, _ = hidden_states.shape
        proj = hidden_states @ in_proj_w.T
        gate, xBC, dt = jnp.split(proj, [INTER, INTER + CONV_DIM], axis=-1)
        xBC_t = jnp.swapaxes(xBC, 1, 2)
        conv = jax.lax.conv_general_dilated(xBC_t, conv_w, window_strides=(1,), padding=[(K - 1, 0)], feature_group_count=CONV_DIM)
        conv = conv + conv_b[None, :, None]
        xBC = jax.nn.silu(jnp.swapaxes(conv, 1, 2))
        x, Bm, Cm = jnp.split(xBC, [INTER, INTER + NG * SS], axis=-1)
        y = _ssd(x.reshape(Bsz, S, NH, HD), Bm.reshape(Bsz, S, NG, SS), Cm.reshape(Bsz, S, NG, SS), D, dt, dt_bias)
        y = y.reshape(Bsz, S, INTER)
        yg = y * jax.nn.silu(gate)
        yg_g = yg.reshape(Bsz, S, NG, GROUP)
        rstd = jax.lax.rsqrt(jnp.mean(jnp.square(yg_g), axis=-1, keepdims=True) + EPS)
        out = (yg_g * rstd).reshape(Bsz, S, INTER) * norm_w
        return out @ out_proj_w.T

    def _L0_ffn_ref(x, W_gate, b_gate, W_e, b_e):
        import jax, jax.numpy as jnp
        import numpy as np
        TOP_K = 2
        logits = x @ W_gate + b_gate
        _, top_idx = jax.lax.top_k(logits, TOP_K)
        y_all = jax.nn.relu(jnp.einsum('bsd,edh->bseh', x, W_e) + b_e)
        y = jnp.take_along_axis(y_all, top_idx[..., None], axis=2)
        return y.mean(axis=2)
    x = x + _L0_xattn_ref(_layernorm(x, axis=-1), ctx_4096, ctx_4096, L0_xattn_Wq, L0_xattn_Wk, L0_xattn_Wv, L0_xattn_Wo)
    x = x + _L0_attn_ref(_layernorm(x, axis=-1), L0_attn_in_proj_w, L0_attn_conv_w, L0_attn_conv_b, L0_attn_dt_bias, L0_attn_D, L0_attn_norm_w, L0_attn_out_proj_w)
    x = x + _L0_ffn_ref(_layernorm(x, axis=-1), L0_ffn_W_gate, L0_ffn_b_gate, L0_ffn_W_e, L0_ffn_b_e)
    return x

_drawn_inputs = setup_inputs


def setup_inputs(seed=0):
    import zlib

    import numpy as np

    out = dict(_drawn_inputs(seed))
    spreads = {'L0_attn_conv_b': (0.0, 0.1),
     'L0_attn_dt_bias': (1.0, 0.6),
     'L0_attn_D': (1.0, 0.2),
     'L0_attn_norm_w': (1.0, 0.2),
     'L0_ffn_b_gate': (0.0, 0.1),
     'L0_ffn_b_e': (0.0, 0.369)}
    factors = {}
    for name, (base, spread) in spreads.items():
        noise = np.random.default_rng([zlib.crc32(name.encode()), seed]).standard_normal(out[name].shape)
        drawn = base * np.exp(spread * noise) if base else spread * noise
        out[name] = jnp.asarray(drawn.astype(out[name].dtype))
    for name, factor in factors.items():
        out[name] = (out[name] * factor).astype(out[name].dtype)
    return out
```

```python
from contextlib import ExitStack

import concourse.bass as bass
from concourse import mybir

F32 = mybir.dt.float32
BF16 = mybir.dt.bfloat16
ALU = mybir.AluOpType
ACT = mybir.ActivationFunctionType
AX = mybir.AxisListType

P = 128
DM = 512
KC = DM // P
SK = 2048
HD = 16
KVH = 8
REP = 4
NKB = SK // P
KCOLS, QCOLS = SK, REP * P
SLOTS = 3
PAIRS = [(0, 0), (0, 1), (0, 2), (1, 0), (1, 1), (2, 0)]
KROWS = HD * len(PAIRS)
MROWS = 2
SCALE = float(HD) ** -0.5
NG = 8
GH = 16
GB = 8
HB = GB // 2
TAPS = 4
PADW = P + TAPS - 1
GROUP = GB * P
NPAR = 8
DT_MIN, DT_MAX = 0.001, 100.0
NE = 8
EPS = 1e-5

C_ID, C_TRI, C_SEG, C_A, C_COMB, C_LT, C_END = 0, 128, 256, 384, 512, 544, 608


def build(nc, d):
    ctx = ExitStack()
    with ctx:
        def sb(name, shape, dt=F32):
            return ctx.enter_context(nc.sbuf_tensor(name, shape, dt))

        def sem(name):
            return ctx.enter_context(nc.semaphore(name))

        res = sb("res", [P, DM])
        xn = sb("xn", [P, DM])
        xT = sb("xT", [P, KC, P])
        cst = sb("cst", [P, C_END])
        identb = sb("identb", [P, P], BF16)
        par = sb("par", [P, NG + 2, GB * NPAR])
        cpar = sb("cpar", [P, GB, NPAR])
        wdt = sb("wdt", [P, KC, P])
        wgate = sb("wgate", [P, KC, NE])
        dtb = sb("dtb", [P, P])
        bgate = sb("bgate", [P, NE])
        dt = sb("dt", [P, P])
        dA = sb("dA", [P, P])
        sqs = sb("sqs", [P, P])
        small = sb("small", [P, 160])
        wx = sb("wx", [P, GB, KC, P])
        wg = sb("wg", [P, GB, KC, P])
        wo = sb("wo", [P, GB * DM])
        wc_v = wo[:, :].rearrange("p (b k f) -> p b k f", b=GB, k=KC)
        wo_v = wo[:, :].rearrange("p (b n) -> p b n", b=GB)
        ps = ctx.enter_context(nc.psum_tensor("ps", [P, 8, 512], F32))

        ident = cst[:, C_ID:C_ID + P]
        tri = cst[:, C_TRI:C_TRI + P]
        segm = cst[:, C_SEG:C_SEG + P]
        acoef = cst[:, C_A:C_A + P]
        comb = cst[:, C_COMB:C_COMB + 32]
        lower = cst[:, C_LT:C_LT + NE * NE].rearrange("p (e j) -> p e j", e=NE)

        stats = small[:, 0:6]
        mean = small[:, 6:7]
        mv2 = small[:, 6:8]
        vareps = small[:, 8:9]
        rstd = small[:, 9:10]
        neghalf = small[:, 10:11]
        ones1 = small[:, 11:12]
        gvar = small[:, 12:13]
        grstd = small[:, 13:14]
        mx = small[:, 16:24]
        nm = small[:, 24:28]
        mparts = small[:, 28:32].bitcast(BF16).rearrange("p (r c) -> p r c", c=2)
        rden = small[:, 32:64]
        lg = small[:, 64:72]
        rank = small[:, 72:80]
        wsel = small[:, 80:88]

        A = sb("arena_a", [P, 20480])
        B = sb("arena_b", [P, 15360])

        def carve(arena, sizes):
            at, out = 0, []
            for n in sizes:
                out.append(arena[:, at:at + n])
                at += n
            assert at <= arena.shape[1], (at, arena.shape)
            return out

        ctx_s, woa_s, pvs_s, pb_s = carve(A, [4 * KC * 512, KC * DM, KVH * 512, 8 * 512])
        ctxT = ctx_s.rearrange("p (t k n) -> p t k n", t=4, k=KC)
        woa = woa_s.rearrange("p (k n) -> p k n", k=KC)
        pvs = pvs_s.rearrange("p (h n) -> p h n", h=KVH)
        pb = pb_s.rearrange("p (b n) -> p b n", b=8)
        resid = pb_s[:, 0:KCOLS + QCOLS]
        we_s, be_s = carve(A, [NE * KC * DM, NE * DM])
        we = we_s.rearrange("p (e k n) -> p e k n", e=NE, k=KC)
        be = be_s.rearrange("p (e n) -> p e n", e=NE)

        (wq_s, wk_s, wv_s, sp_s, kq_s, va_s, vw_s, cs_s) = carve(
            B, [KC * DM, KC * P, KC * P, 3 * (KCOLS + QCOLS) // 2, SLOTS * (KCOLS + QCOLS) // 2,
                NKB * P, SLOTS * NKB * 32, 2 * 512])
        wq = wq_s.rearrange("p (k n) -> p k n", k=KC)
        wk = wk_s.rearrange("p (k n) -> p k n", k=KC)
        wv = wv_s.rearrange("p (k n) -> p k n", k=KC)
        parts = sp_s.bitcast(BF16).rearrange("p (c n) -> p c n", c=3)
        kq = kq_s.bitcast(BF16).rearrange("p (s n) -> p s n", s=SLOTS)
        vall = va_s.rearrange("p (b h c) -> p b h c", b=NKB, h=KVH)
        vw = vw_s.rearrange("p (s b c) -> p s b c", s=SLOTS, b=NKB)
        csb = cs_s.rearrange("p (f n) -> p f n", f=2)
        otok = wq_s[:, 0:DM]

        (pre_s, xs_s, xdt_s, em_s, sg_s, xd_s, yg_s, yw_s, sv_s, bt_s, ct_s, cb_s) = carve(
            B, [GB * PADW, 1024, 1024, 2048, 1024, 1024, 1024, 1024, 1024, 1024, 1024, 1024])
        pre = pre_s.rearrange("p (b n) -> p b n", b=GB)
        xs = xs_s.rearrange("p (b n) -> p b n", b=GB)
        xdt = xdt_s.rearrange("p (h n) -> p h n", h=GH)
        em = em_s.rearrange("p (c h n) -> p c h n", c=4, h=4)
        sg = sg_s.rearrange("p (b n) -> p b n", b=GB)
        xd = xd_s.rearrange("p (b n) -> p b n", b=GB)
        yg = yg_s.rearrange("p (b n) -> p b n", b=GB)
        yw = yw_s.rearrange("p (b n) -> p b n", b=GB)
        sv = sv_s.rearrange("p (c h n) -> p c h n", c=2, h=4)
        bt = bt_s.rearrange("p (g n) -> p g n", g=NG)
        ct = ct_s.rearrange("p (g n) -> p g n", g=NG)
        cbm = cb_s.rearrange("p (g n) -> p g n", g=NG)
        z, nz, ez, ez1, lnz, dz, rz = (em_s[:, n * P:(n + 1) * P] for n in range(7))
        te = xs_s.rearrange("p (b n) -> p b n", b=2)
        re_ = xdt_s.rearrange("p (b n) -> p b n", b=2)
        cmp1 = yg_s[:, 0:64].rearrange("p (e j) -> p e j", e=NE)
        cmp2 = yg_s[:, 64:128].rearrange("p (e j) -> p e j", e=NE)

        ld_x, ld_cst, ld_wq, ld_wk, ld_wv, ld_woa = map(sem, ["ld_x", "ld_cst", "ld_wq", "ld_wk", "ld_wv", "ld_woa"])
        ld_ctx = [sem(f"ld_ctx{t}") for t in range(4)]
        ld_par, ld_wdt, ld_wx, ld_wg, ld_wo, ld_we, ld_be = map(
            sem, ["ld_par", "ld_wdt", "ld_wx", "ld_wg", "ld_wo", "ld_we", "ld_be"])
        ld_kq = [sem(f"ld_kq{s}") for s in range(SLOTS)]
        stored = sem("stored")
        const_set, ident_set = sem("const_set"), sem("ident_set")
        ln_step, rstd_ready, xt_psum, xt_copied = map(sem, ["ln_step", "rstd_ready", "xt_psum", "xt_copied"])
        qk_psum, part1, residual, part2, part3 = map(sem, ["qk_psum", "part1", "residual", "part2", "part3"])
        v_psum, v_copied, vslot_ready = map(sem, ["v_psum", "v_copied", "vslot_ready"])
        row_scores, row_maxed, m_step, m_rows, m_copied = map(
            sem, ["row_scores", "row_maxed", "m_step", "m_rows", "m_copied"])
        scores, probs, pv_groups, pv_saved = map(sem, ["scores", "probs", "pv_groups", "pv_saved"])
        combined, comb_copied_a, comb_copied_v, otr, onorm, attn_psum, attn_added = map(
            sem, ["combined", "comb_copied_a", "comb_copied_v", "otr", "onorm", "attn_psum", "attn_added"])
        dt_psum, dt_step, dt_act = map(sem, ["dt_psum", "dt_step", "dt_act"])
        proj_psum, pre_ready, conv_step, silu_done, cpar_set = map(
            sem, ["proj_psum", "pre_ready", "conv_step", "silu_done", "cpar_set"])
        cb_psum, cb_ready, sv_ready, seg_psum, decay_done, em_ready = map(
            sem, ["cb_psum", "cb_ready", "sv_ready", "seg_psum", "decay_done", "em_ready"])
        xtok_psum, xdt_ready, xd_ready, gate_psum, sg_done, y_psum, u_done, yg_ready = map(
            sem, ["xtok_psum", "xdt_ready", "xd_ready", "gate_psum", "sg_done", "y_psum", "u_done", "yg_ready"])
        sq_done, sqs_ready, ss_psum, gvar_ready, grstd_ready, yw_ready, o_psum, o_added = map(
            sem, ["sq_done", "sqs_ready", "ss_psum", "gvar_ready", "grstd_ready", "yw_ready", "o_psum", "o_added"])
        lg_psum, gate_step, e_psum, t_ready, r_ready, e_added = map(
            sem, ["lg_psum", "gate_step", "e_psum", "t_ready", "r_ready", "e_added"])

        block = ctx.enter_context(nc.Block())

        @block.sync
        def _(sp):
            sp.dma_start(res[:], d["x"]).then_inc(ld_x, 16)
            sp.dma_start(cst[:], d["cst"]).then_inc(ld_cst, 16)
            sp.dma_start(wk, d["wk"]).then_inc(ld_wk, 16)
            sp.dma_start(ctxT[:, 0], d["ctx"][0]).then_inc(ld_ctx[0], 16)
            sp.dma_start(wq, d["wq"]).then_inc(ld_wq, 16)
            for t in range(1, 4):
                sp.dma_start(ctxT[:, t], d["ctx"][t]).then_inc(ld_ctx[t], 16)
            sp.dma_start(wv, d["wv"]).then_inc(ld_wv, 16)

            def stack_parts(i):
                s = i % SLOTS
                rows = slice(HD * i, HD * i + HD)
                for n, (kp, qp) in enumerate(PAIRS):
                    to = slice(HD * n, HD * n + HD)
                    sp.dma_start(kq[to, s, 0:KCOLS], parts[rows, kp, 0:KCOLS]).then_inc(ld_kq[s], 16)
                    sp.dma_start(kq[to, s, KCOLS:], parts[rows, qp, KCOLS:]).then_inc(ld_kq[s], 16)

            sp.wait_ge(part2, 5)
            sp.wait_ge(part3, 5)
            stack_parts(0)
            stack_parts(1)
            sp.dma_start(par[:], d["par"]).then_inc(ld_par, 16)
            sp.dma_start(dtb[:], d["dtb"].to_broadcast([P, P])).then_inc(ld_par, 16)
            sp.dma_start(bgate[:], d["bgate"].to_broadcast([P, NE])).then_inc(ld_par, 16)
            sp.dma_start(woa, d["woa"]).then_inc(ld_woa, 16)
            stack_parts(2)
            sp.dma_start(wdt[:], d["wdt"]).then_inc(ld_wdt, 16)
            sp.dma_start(wgate[:], d["wgate"]).then_inc(ld_wdt, 16)
            sp.dma_start(wg[:], d["wbc"][0]).then_inc(ld_wg, 16)
            for i in range(SLOTS, KVH):
                sp.wait_ge(scores, NKB * (i - 2))
                stack_parts(i)
                if i == SLOTS:
                    sp.dma_start(wc_v, d["wbc"][1]).then_inc(ld_wo, 16)
                if i == SLOTS + 1:
                    sp.dma_start(wx[:], d["wx"][0]).then_inc(ld_wx, 16)
            sp.wait_ge(attn_psum, 1)
            sp.dma_start(be_s, d["be"].to_broadcast([P, NE * DM])).then_inc(ld_be, 16)
            sp.wait_ge(proj_psum, 2)
            sp.dma_start(wg[:], d["wg"][0]).then_inc(ld_wg, 16)
            sp.wait_ge(proj_psum, 4)
            sp.dma_start(wo_v, d["wout"][0]).then_inc(ld_wo, 16)

            def reload(g, first=False, last=False):
                if not last:
                    sp.wait_ge(proj_psum, g * 2 + 6)
                    sp.dma_start(wx[:], d["wx"][bass.ds(g + 1, 1)].rearrange("o p b k f -> (o p) b k f")
                                 ).then_inc(ld_wx, 16)
                sp.dma_start(we[:, bass.ds(g, 1)].rearrange("p o k n -> p (o k) n"),
                             d["we"][bass.ds(g, 1)].rearrange("o p k n -> (o p) k n")).then_inc(ld_we, 16)
                if not first:
                    sp.wait_ge(o_psum, g)
                    sp.dma_start(wo_v, d["wout"][bass.ds(g, 1)].rearrange("o p b n -> (o p) b n")
                                 ).then_inc(ld_wo, 16)
                if not last:
                    sp.wait_ge(gate_psum, g * 2 + 2)
                    sp.dma_start(wg[:], d["wg"][bass.ds(g + 1, 1)].rearrange("o p b k f -> (o p) b k f")
                                 ).then_inc(ld_wg, 16)

            reload(0, first=True)
            with sp.Fori(1, NG - 1) as g:
                reload(g)
            reload(NG - 1, last=True)
            sp.wait_ge(e_added, NE)
            sp.dma_start(d["out"], res[:]).then_inc(stored, 16)
            sp.wait_ge(stored, 16)

        @block.gpsimd
        def _(pool):
            fills = [(neghalf, -0.5), (ones1, 1.0), (vw[:, :, :, HD:32], 1.0)]
            fills += [(kq[KROWS:KROWS + MROWS, s, 0:KCOLS], 1.0) for s in range(SLOTS)]
            for n, (what, value) in enumerate(fills):
                if n:
                    pool.wait_ge(const_set, n)
                pool.memset(what, value).then_inc(const_set, 1)

            def rstd_of(n):
                pool.wait_ge(ln_step, n * 4 + 3)
                pool.tensor_tensor(rstd, vareps, neghalf, ALU.pow).then_inc(rstd_ready, 1)

            pool.wait_ge(const_set, 6)
            rstd_of(0)

            def v_slot(i, s):
                pool.tensor_copy(vw[:, s, :, 0:HD],
vall[:, :, i, :]).then_inc(vslot_ready, 1)

            pool.wait_ge(v_copied, 4)
            for i in range(SLOTS):
                v_slot(i, i)
            for i in range(SLOTS, KVH):
                pool.wait_ge(pv_groups, 4 * (i - SLOTS) + 4)
                v_slot(i, i % SLOTS)
            rstd_of(1)

            def conv_params(n):
                pool.tensor_copy(cpar[:], par[:, bass.ds(n, 1), :].rearrange("p o (b c) -> p (o b) c", c=NPAR)
                                 ).then_inc(cpar_set, 1)

            pool.wait_ge(ld_par, 48)
            conv_params(0)
            for n in (1, 2):
                pool.wait_ge(conv_step, n * 32)
                conv_params(n)

            def masked_dA(g, c, wait):
                if wait:
                    pool.wait_ge(seg_psum, g * 4 + c - 1)
                pool.tensor_tensor(
                    sv[:, c % 2], tri.unsqueeze(1).to_broadcast([P, 4, P]),
                    dA[:, bass.ds(g * GH + c * 4, 4)].unsqueeze(2).to_broadcast([P, 4, P]),
                    ALU.mult).then_inc(sv_ready, 1)

            def skip_term(g, first=False):
                pool.wait_ge(silu_done, g * 2 + 6)
                if not first:
                    pool.wait_ge(sqs_ready, g)
                dcol = par[:, bass.ds(g + 2, 1), :].rearrange("p o (b c) -> p (o b) c", c=NPAR)[:, :, 5:6]
                pool.tensor_tensor(xd, xs, dcol.to_broadcast([P, GB, P]), ALU.mult).then_inc(xd_ready, 1)

            def norm_weight(g, first=False):
                pool.wait_ge(yg_ready, g * 2 + 2)
                if not first:
                    pool.wait_ge(o_psum, g)
                wcol = par[:, bass.ds(g + 2, 1), :].rearrange("p o (b c) -> p (o b) c", c=NPAR)[:, :, 6:7]
                pool.tensor_tensor(yw, yg, wcol.to_broadcast([P, GB, P]), ALU.mult).then_inc(yw_ready, 1)

            def group_rstd(g):
                pool.wait_ge(gvar_ready, g + 1)
                pool.tensor_tensor(grstd, gvar, neghalf, ALU.pow).then_inc(grstd_ready, 1)

            def group(g, first=False, last=False):
                if not first:
                    norm_weight(g - 1, first=isinstance(g, int) and g == 1)
                for c in (0, 1):
                    masked_dA(g, c, wait=not first)
                if not first:
                    group_rstd(g - 1)
                for c in (2, 3):
                    masked_dA(g, c, wait=True)
                skip_term(g, first)
                if not last:
                    pool.wait_ge(conv_step, g * 32 + 96)
                    conv_params(g + 3)

            pool.wait_ge(dt_step, 10)
            group(0, first=True)
            group(1)
            with pool.Fori(2, NG - 1) as g:
                group(g)
            group(NG - 1, last=True)
            norm_weight(NG - 1)
            group_rstd(NG - 1)
            rstd_of(2)

        @block.scalar
        def _(act):
            def chunk(n):
                return slice(KCOLS, KCOLS + QCOLS) if n == 0 else slice(512 * (n - 1), n * 512)

            def bank(n):
                return 7 if n == 0 else n - 1

            def second_part(n):
                act.wait_ge(residual, n + 1)
                act.activation(parts[:, 1, chunk(n)], resid[:, chunk(n)], ACT.Copy).then_inc(part2, 1)

            for n in range(5):
                act.wait_ge(qk_psum, n + 1)
                act.activation(parts[:, 0, chunk(n)], ps[:, bank(n), :], ACT.Copy).then_inc(part1, 1)
                if n:
                    second_part(n - 1)
            second_part(4)
            for t in range(4):
                act.wait_ge(v_psum, t + 1)
                act.activation(vall[:, t * 4:t * 4 + 4], ps[:, 4 + t % 2, :].rearrange(
                    "p (b h c) -> p b h c", b=4, h=KVH), ACT.Copy).then_inc(v_copied, 1)

            def attend(i, s, first=False):
                act.wait_ge(m_rows, i + 1)
                act.activation(kq[KROWS:KROWS + MROWS, s, KCOLS:], ps[KROWS:KROWS + MROWS, 7, :],
                               ACT.Copy).then_inc(m_copied, 1)
                for b in range(NKB):
                    if b == 4 and not first:
                        save_pv(i - 1)
                    act.wait_ge(scores, i * NKB + b + 1)
                    if not first or b >= 8:
                        act.wait_ge(pv_groups, i * 4 + b // 4 - 1)
                    act.activation(pb[:, b % 8], ps[:, 4 + b % 2, :], ACT.Exp, scale=SCALE).then_inc(probs, 1)

            def save_pv(i):
                act.wait_ge(pv_groups, i * 4 + 4)
                act.activation(pvs[:, bass.ds(i, 1)].rearrange("p o n -> p (o n)"), ps[:, 6, :],
                               ACT.Copy).then_inc(pv_saved, 1)

            attend(0, 0, first=True)
            with act.Fori(0, 2) as t:
                for u in range(3):
                    attend(t * 3 + (1 + u), (1 + u) % SLOTS)
            attend(KVH - 1, (KVH - 1) % 3)
            save_pv(KVH - 1)
            act.wait_ge(combined, 1)
            act.activation(csb[:, 0], ps[:, 0, :], ACT.Copy).then_inc(comb_copied_a, 1)

            act.wait_ge(dt_step, 2)
            act.activation(ez, nz, ACT.Exp).then_inc(dt_act, 1)
            act.wait_ge(dt_step, 3)
            act.activation(lnz, ez1, ACT.Ln).then_inc(dt_act, 1)

            def evacuate(n, banks, first=False):
                for h in range(2):
                    act.wait_ge(proj_psum, n * 2 + h + 1)
                    if not first:
                        act.wait_ge(conv_step, n * 32 - 16 + 16 * h)
                    act.activation(pre[:, HB * h:HB * h + HB, TAPS - 1:],
                                   ps[:, banks + h, :].rearrange("p (b n) -> p b n", b=HB),
                                   ACT.Copy).then_inc(pre_ready, 1)

            def silu(n, to):
                for h in range(2):
                    act.wait_ge(conv_step, n * 32 + 16 * h + 16)
                    act.activation(to[:, HB * h:HB * h + HB], xs[:, HB * h:HB * h + HB],
                                   ACT.Silu).then_inc(silu_done, 1)

            evacuate(0, 0, first=True)
            silu(0, bt)
            evacuate(1, 2)
            silu(1, ct)

            def square(g):
                act.wait_ge(yg_ready, g * 2 + 2)
                act.activation(xd, yg, ACT.Square).then_inc(sq_done, 1)

            def group(g, first=False):
                if not first:
                    square(g - 1)
                evacuate(g + 2, 0)
                silu(g + 2, xs)
                if not first:
                    act.wait_ge(y_psum, g * 2)
                for c in range(4):
                    act.wait_ge(seg_psum, g * 4 + c + 1)
                    act.activation(em[:, c], ps[:, 4 + c % 2, :].rearrange("p (h n) -> p h n", h=4),
                                   ACT.Exp).then_inc(decay_done, 1)
                if not first:
                    act.wait_ge(yg_ready, g * 2)
                for h in range(2):
                    act.wait_ge(gate_psum, g * 2 + h + 1)
                    act.activation(sg[:, HB * h:HB * h + HB],
                                   ps[:, 2 + h, :].rearrange("p (b n) -> p b n", b=HB),
                                   ACT.Silu).then_inc(sg_done, 1)

            group(0, first=True)
            with act.Fori(1, NG) as g:
                group(g)
            square(NG - 1)

            def expert(e, s, first=False):
                act.wait_ge(t_ready, e + 1)
                if not first:
                    act.wait_ge(e_added, e - 1)
                act.activation(re_[:, s], te[:, s], ACT.Relu,
                               scale=wsel[:, bass.ds(e, 1)]).then_inc(r_ready, 1)

            act.wait_ge(gate_step, 7)
            for e in (0, 1):
                expert(e, e, first=True)
            with act.Fori(1, NE // 2) as pair:
                for u in range(2):
                    expert(pair * 2 + u, u)

        @block.vector
        def _(dve):
            def layer_norm(n):
                dve.bn_stats(stats, res[:]).then_inc(ln_step, 1)
                dve.wait_ge(ln_step, n * 4 + 1)
                dve.bn_aggr(mv2, stats).then_inc(ln_step, 1)
                dve.wait_ge(ln_step, n * 4 + 2)
                dve.tensor_scalar(vareps, small[:, 7:8], EPS, None, ALU.add).then_inc(ln_step, 1)
                dve.wait_ge(rstd_ready, n + 1)
                dve.tensor_scalar(xn[:], res[:], mean, rstd, ALU.subtract, ALU.mult).then_inc(ln_step, 1)

            def take_transposed(n, bank):
                dve.wait_ge(xt_psum, n + 1)
                dve.tensor_copy(xT[:], ps[:, bank, :].rearrange("p (k n) -> p k n", k=KC)).then_inc(xt_copied, 1)

            dve.wait_ge(ld_x, 16)
            layer_norm(0)
            dve.wait_ge(ld_cst, 16)
            dve.tensor_copy(identb[:], ident).then_inc(ident_set, 1)
            take_transposed(0, 6)

            def chunk(n):
                return slice(KCOLS, KCOLS + QCOLS) if n == 0 else slice(512 * (n - 1), n * 512)

            def bank(n):
                return 7 if n == 0 else n - 1

            def third_part(n):
                dve.wait_ge(part2, n + 1)
                dve.tensor_tensor(parts[:, 2, chunk(n)], resid[:, chunk(n)], parts[:, 1, chunk(n)],
                                  ALU.subtract).then_inc(part3, 1)

            for n in range(5):
                dve.wait_ge(part1, n + 1)
                dve.tensor_tensor(resid[:, chunk(n)], ps[:, bank(n), :], parts[:, 0, chunk(n)],
                                  ALU.subtract).then_inc(residual, 1)
                if n:
                    third_part(n - 1)
            third_part(4)

            def maxima(i, first=False):
                for c in range(8):
                    dve.wait_ge(row_scores, i * 8 + c + 1)
                    dve.tensor_reduce(mx[:, c:c + 1], ps[:, 2 * (c % 2):2 * (c % 2) + 2, :],
                                      AX.XY, ALU.max).then_inc(row_maxed, 1)
                dve.wait_ge(row_maxed, i * 8 + 8)
                dve.tensor_reduce(nm, mx.rearrange("p (r c) -> p r c", c=2), AX.X, ALU.max,
                                  negate=True).then_inc(m_step, 1)
                dve.wait_ge(m_step, i * 3 + 1)
                if not first:
                    dve.wait_ge(m_rows, i)
                dve.tensor_copy(mparts[:, :, 0], nm).then_inc(m_step, 1)
                dve.wait_ge(m_step, i * 3 + 2)
                dve.tensor_tensor(mparts[:, :, 1], nm, mparts[:, :, 0], ALU.subtract).then_inc(m_step, 1)

            maxima(0, first=True)
            with dve.Fori(1, KVH) as i:
                maxima(i)

            dve.wait_ge(combined, 2)
            dve.tensor_copy(csb[:, 1], ps[:, 1, :]).then_inc(comb_copied_v, 1)
            dve.wait_ge(otr, 2)
            both = ps[:, 2:4, :].rearrange("p f (r j c) -> p f r j c", r=REP, j=4)
            dve.reciprocal(rden.rearrange("p (n o) -> p n o", o=1),
                           ps[:, 2:4, :].rearrange("p f (n c) -> p (f n) c", c=32)[:, :, HD:HD + 1]
                           ).then_inc(onorm, 1)
            dve.wait_ge(onorm, 1)
            for f in range(2):
                dve.tensor_tensor(
                    otok[:, 256 * f:256 * f + 256].rearrange("p (j r c) -> p r j c", j=4, r=REP),
                    both[:, f, :, :, 0:HD],
                    rden[:, 16 * f:16 * f + 16].rearrange("p (r j) -> p r j", r=REP).unsqueeze(3)
                    .to_broadcast([P, REP, 4, HD]), ALU.mult).then_inc(onorm, 1)
            take_transposed(1, 4)
            dve.wait_ge(attn_psum, 1)
            dve.tensor_tensor(res[:], ps[:, 5, :], res[:], ALU.add).then_inc(attn_added, 1)
            dve.wait_ge(attn_added, 1)
            layer_norm(1)
            dve.memset(pre[:, :, 0:TAPS - 1], 0.0)
            take_transposed(2, 6)

            def step(n):
                dve.wait_ge(dt_step, n)

            dve.wait_ge(dt_psum, 1)
            dve.wait_ge(ld_par, 48)
            dve.tensor_tensor(z, ps[:, 7, 0:P], dtb[:], ALU.add).then_inc(dt_step, 1)
            step(1)
            dve.scalar_tensor_tensor(nz, z, -1.0, z, ALU.mult, ALU.min).then_inc(dt_step, 1)
            dve.wait_ge(dt_act, 1)
            dve.tensor_scalar(ez1, ez, 1.0, None, ALU.add).then_inc(dt_step, 1)
            step(3)
            dve.tensor_scalar(dz, ez1, -1.0, 1e-30, ALU.add, ALU.max).then_inc(dt_step, 1)
            step(4)
            dve.reciprocal(rz, dz).then_inc(dt_step, 1)
            step(5)
            dve.tensor_tensor(rz, rz, ez, ALU.mult).then_inc(dt_step, 1)
            step(6)
            dve.wait_ge(dt_act, 2)
            dve.tensor_tensor(rz, rz, lnz, ALU.mult).then_inc(dt_step, 1)
            step(7)
            dve.scalar_tensor_tensor(dt[:], z, 0.0, rz, ALU.max, ALU.add).then_inc(dt_step, 1)
            step(8)
            dve.tensor_scalar(dt[:], dt[:], DT_MIN, DT_MAX, ALU.max, ALU.min).then_inc(dt_step, 1)
            step(9)
            dve.tensor_tensor(dA[:], dt[:], acoef, ALU.mult).then_inc(dt_step, 1)

            def conv(n, h):
                dve.wait_ge(pre_ready, n * 2 + h + 1)
                for k in reversed(range(TAPS)):
                    for b in range(HB * h, HB * h + HB):
                        done = n * 32 + 16 * h + HB * (TAPS - 1 - k) + b - HB * h
                        if k == TAPS - 1:
                            dve.tensor_scalar(xs[:, b], pre[:, b, k:k + P], cpar[:, b, k:k + 1],
                                              cpar[:, b, 4:5], ALU.mult, ALU.add).then_inc(conv_step, 1)
                        else:
                            dve.wait_ge(conv_step, done - HB + 1)
                            dve.scalar_tensor_tensor(xs[:, b], pre[:, b, k:k + P], cpar[:, b, k:k + 1],
                                                     xs[:, b], ALU.mult, ALU.add).then_inc(conv_step, 1)

            for n in (0, 1):
                dve.wait_ge(cpar_set, n + 1)
                if n:
                    dve.wait_ge(silu_done, 2)
                for h in range(2):
                    conv(n, h)

            def masked_cb():
                for h in range(2):
                    dve.wait_ge(cb_psum, h + 1)
                    dve.tensor_tensor(cbm[:, 4 * h:4 * h + 4],
                                      ps[:, 4 + h, :].rearrange("p (g n) -> p g n", g=4),
                                      tri.unsqueeze(1).to_broadcast([P, 4, P]), ALU.mult).then_inc(cb_ready, 1)

            def gated(g, first=False):
                dve.wait_ge(xd_ready, g + 1)
                if not first:
                    dve.wait_ge(sq_done, g)
                    dve.wait_ge(yw_ready, g)
                for h in range(2):
                    dve.wait_ge(y_psum, g * 2 + h + 1)
                    dve.tensor_tensor(yg[:, HB * h:HB * h + HB],
                                      ps[:, 4 + h, :].rearrange("p (b n) -> p b n", b=HB),
                                      xd[:, HB * h:HB * h + HB], ALU.add).then_inc(u_done, 1)
                dve.wait_ge(sg_done, g * 2 + 2)
                for h in range(2):
                    dve.wait_ge(u_done, g * 2 + h + 1)
                    dve.tensor_tensor(yg[:, HB * h:HB * h + HB], yg[:, HB * h:HB * h + HB],
                                      sg[:, HB * h:HB * h + HB], ALU.mult).then_inc(yg_ready, 1)

            def sum_squares(g, first=False):
                dve.wait_ge(sq_done, g + 1)
                if not first:
                    dve.wait_ge(ss_psum, g)
                dve.tensor_reduce(sqs[:], xd.rearrange("p b n -> p n b"), AX.X, ALU.add).then_inc(sqs_ready, 1)

            def group_variance(g):
                dve.wait_ge(ss_psum, g + 1)
                dve.tensor_scalar(gvar, ps[:, 7, 0:1], 1.0 / GROUP, EPS, ALU.mult, ALU.add).then_inc(gvar_ready, 1)

            def add_group(g):
                dve.wait_ge(grstd_ready, g + 1)
                dve.wait_ge(o_psum, g + 1)
                dve.scalar_tensor_tensor(res[:], ps[:, 6, :], grstd, res[:], ALU.mult, ALU.add).then_inc(o_added, 1)

            def group(g, first=False, second=False):
                if not first:
                    gated(g - 1, first=second)
                    sum_squares(g - 1, first=second)
                dve.wait_ge(cpar_set, g + 3)
                if first:
                    dve.wait_ge(silu_done, 4)
                else:
                    dve.wait_ge(xtok_psum, g * 2)
                    dve.wait_ge(xd_ready, g)
                for h in range(2):
                    conv(g + 2, h)
                if first:
                    masked_cb()
                    dve.wait_ge(cb_ready, 2)
                else:
                    group_variance(g - 1)
                for c in range(4):
                    dve.wait_ge(decay_done, g * 4 + c + 1)
                    dve.tensor_tensor(em[:, c], em[:, c], cbm[:, bass.ds(g, 1)].to_broadcast([P, 4, P]),
                                      ALU.mult).then_inc(em_ready, 1)
                if not first:
                    add_group(g - 1)
                for h in range(2):
                    dve.wait_ge(xtok_psum, g * 2 + h + 1)
                    dve.tensor_tensor(
                        xdt[:, GB * h:GB * h + GB], ps[:, h, :].rearrange("p (n c) -> p n c", n=8),
                        dt[:, bass.ds(g * GH + GB * h, GB)].unsqueeze(2).to_broadcast([P, GB, 64]),
                        ALU.mult).then_inc(xdt_ready, 1)

            group(0, first=True)
            group(1, second=True)
            with dve.Fori(2, NG) as g:
                group(g)
            gated(NG - 1)
            sum_squares(NG - 1)
            group_variance(NG - 1)
            add_group(NG - 1)
            dve.wait_ge(o_added, NG)

            layer_norm(2)
            take_transposed(3, 6)
            dve.wait_ge(lg_psum, 1)
            dve.tensor_tensor(lg, ps[:, 7, 0:NE], bgate[:], ALU.add).then_inc(gate_step, 1)
            dve.wait_ge(gate_step, 1)
            lg_j = lg.unsqueeze(1).to_broadcast([P, NE, NE])
            lg_e = lg.unsqueeze(2).to_broadcast([P, NE, NE])
            dve.tensor_tensor(cmp1, lg_j, lg_e, ALU.is_gt).then_inc(gate_step, 1)
            dve.tensor_tensor(cmp2, lg_j, lg_e, ALU.is_equal).then_inc(gate_step, 1)
            dve.wait_ge(gate_step, 3)
            dve.tensor_tensor(cmp2, cmp2, lower, ALU.mult).then_inc(gate_step, 1)
            dve.wait_ge(gate_step, 4)
            dve.tensor_tensor(cmp1, cmp1, cmp2, ALU.add).then_inc(gate_step, 1)
            dve.wait_ge(gate_step, 5)
            dve.tensor_reduce(rank, cmp1, AX.X, ALU.add).then_inc(gate_step, 1)
            dve.wait_ge(gate_step, 6)
            dve.tensor_scalar(wsel, rank, 1.5, 0.5, ALU.is_lt, ALU.mult).then_inc(gate_step, 1)

            def add_bias(e, s, first=False):
                dve.wait_ge(e_psum, e + 1)
                if not first:
                    dve.wait_ge(r_ready, e - 1)
                dve.tensor_tensor(te[:, s], ps[:, s, :], be[:, bass.ds(e, 1)].rearrange("p o n -> p (o n)"),
                                  ALU.add).then_inc(t_ready, 1)

            def add_expert(e, s, first=False):
                dve.wait_ge(r_ready, e + 1)
                if not first:
                    dve.wait_ge(e_added, e)
                dve.tensor_tensor(res[:], res[:], re_[:, s], ALU.add).then_inc(e_added, 1)

            dve.wait_ge(ld_be, 16)
            add_bias(0, 0, first=True)
            add_bias(1, 1, first=True)
            add_expert(0, 0, first=True)
            with dve.Fori(1, NE // 2) as pair:
                for u in range(2):
                    add_bias(pair * 2 + u, u)
                    add_expert(pair * 2 + u - 1, 1 - u)
            add_expert(NE - 1, 1)

        @block.tensor
        def _(pe):
            def transpose_xn(n, src, bank):
                for k in range(KC):
                    last = pe.transpose(ps[:, bank, P * k:P * k + P], src[:, P * k:P * k + P], ident)
                last.then_inc(xt_psum, 1)

            pe.wait_ge(ld_cst, 16)
            pe.wait_ge(ln_step, 4)
            transpose_xn(0, xn, 6)
            pe.wait_ge(xt_copied, 1)
            pe.wait_ge(ld_wq, 16)
            for r in range(REP):
                for k in range(KC):
                    last = pe.matmul(ps[:, 7, P * r:P * r + P], wq[:, k, P * r:P * r + P], xT[:, k],
                                     start=k == 0, stop=k == KC - 1)
            last.then_inc(qk_psum, 1)
            pe.wait_ge(ld_wk, 16)
            for t in range(4):
                pe.wait_ge(ld_ctx[t], 16)
                for k in range(KC):
                    last = pe.matmul(ps[:, t, :], wk[:, k], ctxT[:, t, k], start=k == 0, stop=k == KC - 1)
                last.then_inc(qk_psum, 1)
            pe.wait_ge(ld_wv, 16)
            for t in range(4):
                if t >= 2:
                    pe.wait_ge(v_copied, t - 1)
                for b in range(4):
                    for k in range(KC):
                        last = pe.matmul(ps[:, 4 + t % 2, P * b:P * b + P], ctxT[:, t, k, P * b:P * b + P],
                                         wv[:, k], start=k == 0, stop=k == KC - 1)
                last.then_inc(v_psum, 1)

            def rows(i, s, c, first=False):
                if not first:
                    pe.wait_ge(row_maxed, i * 8 + c - 1)
                r, half = c // 2, c % 2
                for j in range(2):
                    at = 1024 * half + 512 * j
                    last = pe.matmul(ps[:, 2 * (c % 2) + j, :], kq[0:KROWS, s, KCOLS + P * r:KCOLS + P * r + P],
                                     kq[0:KROWS, s, at:at + 512], start=True, stop=True)
                last.then_inc(row_scores, 1)

            def maxima_to_rows(i, s):
                pe.wait_ge(m_step, i * 3 + 3)
                for r in range(REP):
                    last = pe.matmul(ps[KROWS:KROWS + MROWS, 7, P * r:P * r + P], mparts[:, r], identb[:],
                                     start=True, stop=True, tile_position=(0, KROWS))
                last.then_inc(m_rows, 1)

            def columns(i, s, b, first=False):
                if b == 0:
                    pe.wait_ge(m_copied, i + 1)
                if not (first and b < 2):
                    pe.wait_ge(probs, i * NKB + b - 1)
                pe.matmul(ps[:, 4 + b % 2, :], kq[0:KROWS + MROWS, s, P * b:P * b + P],
                          kq[0:KROWS + MROWS, s, KCOLS:], start=True, stop=True).then_inc(scores, 1)

            def product(i, s, grp, first=False):
                pe.wait_ge(probs, i * NKB + 4 * grp + 4)
                if grp == 0:
                    pe.wait_ge(vslot_ready, i + 1)
                    if not first:
                        pe.wait_ge(pv_saved, i)
                for j in range(4):
                    last = pe.matmul(ps[32 * j:32 * j + 32, 6, :], vw[:, s, 4 * grp + j], pb[:, (4 * grp + j) % 8],
                                     start=grp == 0, stop=grp == 3, tile_position=(0, 32 * j))
                last.then_inc(pv_groups, 1)

            pe.wait_ge(const_set, 6)
            pe.wait_ge(part3, 5)
            pe.wait_ge(ld_kq[0], 192)
            for c in range(8):
                rows(0, 0, c, first=c < 2)
            pe.wait_ge(ident_set, 1)
            pe.wait_ge(v_copied, 4)

            def stage(i, s, t=None, u=None, **kw):
                n = (s + 1) % SLOTS
                turns = (u + 2) // SLOTS + 1 if t is not None else (i + 1) // SLOTS + 1

                def ahead(c):
                    if kw.get("last"):
                        return
                    if c == 0:
                        pe.wait_ge(ld_kq[n], 192 * turns if t is None else t * 192 + 192 * turns)
                    rows(i + 1, n, c)

                first = kw.get("first", False)
                ahead(0)
                if not first:
                    product(i - 1, (s + 2) % SLOTS, 3, first=False)
                maxima_to_rows(i, s)
                for b in range(NKB):
                    columns(i, s, b, first)
                    if b % 2 == 1 and (b + 1) // 2 <= 7:
                        ahead((b + 1) // 2)
                    if b in (5, 9, 13):
                        product(i, s, (b - 5) // 4, first)

            stage(0, 0, first=True)
            with pe.Fori(0, 2) as t:
                for u in range(3):
                    stage(t * 3 + (1 + u), (1 + u) % SLOTS, t=t, u=u)
            stage(KVH - 1, (KVH - 1) % SLOTS, last=True)
            product(KVH - 1, (KVH - 1) % SLOTS, 3)

            pe.wait_ge(pv_saved, KVH)
            for f in range(2):
                for j in range(4):
                    last = pe.matmul(ps[32 * j:32 * j + 32, f, :], comb, pvs[:, 4 * f + j],
                                     start=True, stop=True, tile_position=(0, 32 * j))
                last.then_inc(combined, 1)
            for f in range(2):
                pe.wait_ge((comb_copied_a, comb_copied_v)[f], 1)
                for r in range(REP):
                    last = pe.transpose(ps[:, 2 + f, P * r:P * r + P], csb[:, f, P * r:P * r + P], ident)
                last.then_inc(otr, 1)
            pe.wait_ge(onorm, 3)
            transpose_xn(1, otok, 4)
            pe.wait_ge(xt_copied, 2)
            pe.wait_ge(ld_woa, 16)
            for k in range(KC):
                last = pe.matmul(ps[:, 5, :], xT[:, k], woa[:, k], start=k == 0, stop=k == KC - 1)
            last.then_inc(attn_psum, 1)

            pe.wait_ge(ln_step, 8)
            transpose_xn(2, xn, 6)
            pe.wait_ge(xt_copied, 3)
            pe.wait_ge(ld_wdt, 32)
            for k in range(KC):
                last = pe.matmul(ps[:, 7, 0:P], xT[:, k], wdt[:, k], start=k == 0, stop=k == KC - 1)
            last.then_inc(dt_psum, 1)

            def project(w, banks, done):
                for b in range(GB):
                    for k in range(KC):
                        last = pe.matmul(ps[:, banks + b // HB, P * (b % HB):P * (b % HB) + P],
                                         w[:, b, k], xT[:, k], start=k == 0, stop=k == KC - 1)
                    if b % HB == HB - 1:
                        last.then_inc(done, 1)

            pe.wait_ge(ld_wg, 16)
            project(wg, 0, proj_psum)
            pe.wait_ge(ld_wo, 16)
            project(wc_v, 2, proj_psum)

            def out_proj(g, first=False):
                pe.wait_ge(sqs_ready, g + 1)
                pe.matmul(ps[:, 7, 0:1], sqs[:], ones1, start=True, stop=True).then_inc(ss_psum, 1)
                pe.wait_ge(ld_wo, g * 16 + 32)
                pe.wait_ge(yw_ready, g + 1)
                if not first:
                    pe.wait_ge(o_added, g)
                for b in range(GB):
                    last = pe.matmul(ps[:, 6, :], yw[:, b], wo_v[:, b], start=b == 0, stop=b == GB - 1)
                last.then_inc(o_psum, 1)

            def group(g, first=False, second=False):
                pe.wait_ge(ld_wx, g * 16 + 16)
                if first:
                    pe.wait_ge(pre_ready, 2)
                else:
                    pe.wait_ge(xdt_ready, g * 2)
                project(wx, 0, proj_psum)
                if first:
                    pe.wait_ge(silu_done, 4)
                    for n in range(NG):
                        last = pe.matmul(ps[:, 4 + n // 4, P * (n % 4):P * (n % 4) + P], bt[:, n], ct[:, n],
                                         start=True, stop=True)
                        if n % 4 == 3:
                            last.then_inc(cb_psum, 1)
                    pe.wait_ge(cb_ready, 2)
                else:
                    out_proj(g - 1, first=second)
                    pe.wait_ge(u_done, g * 2)
                for c in range(4):
                    pe.wait_ge(sv_ready, g * 4 + c + 1)
                    if c >= 2:
                        pe.wait_ge(decay_done, g * 4 + c - 1)
                    pe.matmul(ps[:, 4 + c % 2, :], segm, sv[:, c % 2], start=True, stop=True).then_inc(seg_psum, 1)
                for h in range(2):
                    pe.wait_ge(silu_done, g * 2 + h + 5)
                    for b in range(HB):
                        last = pe.transpose(ps[:, h, P * b:P * b + P], xs[:, HB * h + b], ident)
                    last.then_inc(xtok_psum, 1)
                pe.wait_ge(ld_wg, g * 16 + 32)
                if first:
                    pe.wait_ge(pre_ready, 4)
                else:
                    pe.wait_ge(sg_done, g * 2)
                project(wg, 2, gate_psum)
                pe.wait_ge(em_ready, g * 4 + 4)
                pe.wait_ge(xdt_ready, g * 2 + 2)
                for b in range(GB):
                    for o in range(2):
                        h = 2 * b + o
                        last = pe.matmul(ps[64 * o:64 * o + 64, 4 + b // HB, P * (b % HB):P * (b % HB) + P],
                                         xdt[:, h], em[:, h // 4, h % 4], start=True, stop=True,
                                         tile_position=(0, 64 * o))
                    if b % HB == HB - 1:
                        last.then_inc(y_psum, 1)

            group(0, first=True)
            group(1, second=True)
            with pe.Fori(2, NG) as g:
                group(g)
            out_proj(NG - 1)

            pe.wait_ge(ln_step, 12)
            transpose_xn(3, xn, 6)
            pe.wait_ge(xt_copied, 4)
            for k in range(KC):
                last = pe.matmul(ps[:, 7, 0:NE], xT[:, k], wgate[:, k], start=k == 0, stop=k == KC - 1)
            last.then_inc(lg_psum, 1)
            pe.wait_ge(ld_we, 16 * NE)

            def expert(e, s, first=False):
                if not first:
                    pe.wait_ge(t_ready, e - 1)
                for k in range(KC):
                    last = pe.matmul(ps[:, s, :], xT[:, k], we[:, bass.ds(e, 1), k].rearrange("p o n -> p (o n)"),
                                     start=k == 0, stop=k == KC - 1)
                last.then_inc(e_psum, 1)

            for e in (0, 1):
                expert(e, e, first=True)
            with pe.Fori(1, NE // 2) as pair:
                for u in range(2):
                    expert(pair * 2 + u, u)


def kernel(x, ctx_4096, L0_xattn_Wq, L0_xattn_Wk, L0_xattn_Wv, L0_xattn_Wo, L0_attn_in_proj_w,
           L0_attn_conv_w, L0_attn_conv_b, L0_attn_dt_bias, L0_attn_D, L0_attn_norm_w,
           L0_attn_out_proj_w, L0_ffn_W_gate, L0_ffn_b_gate, L0_ffn_W_e, L0_ffn_b_e):
    import numpy as np
    import concourse.bacc as bacc
    from concourse.bass_utils import run_bass_kernel_spmd

    f = np.float32
    inter = NG * GROUP
    a = {}

    def by_partition(w):
        return w.reshape(KC, P, w.shape[-1]).transpose(1, 0, 2)

    i = np.arange(P)
    cst = np.zeros((P, C_END), f)
    cst[:, C_ID:C_ID + P] = np.eye(P)
    cst[:, C_TRI:C_TRI + P] = i[:, None] <= i[None, :]
    cst[:, C_SEG:C_SEG + P] = i[:, None] > i[None, :]
    cst[:, C_A:C_A + P] = -(i[None, :] + 1.0)
    cst[:, C_COMB:C_COMB + HD] = (i % 32)[:, None] == np.arange(HD)[None, :]
    cst[:, C_COMB + HD:C_COMB + 32] = ((i % 32) == HD)[:, None]
    cst[:, C_LT:C_END] = np.tril(np.ones((NE, NE)), -1).ravel()[None, :]
    a["cst"] = cst

    a["x"] = np.asarray(x).reshape(P, DM)
    a["ctx"] = np.asarray(ctx_4096).reshape(4, 512, KC, P).transpose(0, 3, 2, 1)
    wq = np.asarray(L0_xattn_Wq).reshape(DM, KVH, REP, HD).transpose(0, 2, 1, 3).reshape(DM, DM)
    a["wq"] = by_partition(wq)
    a["wk"] = by_partition(np.asarray(L0_xattn_Wk))
    a["wv"] = by_partition(np.asarray(L0_xattn_Wv))
    a["woa"] = by_partition(np.asarray(L0_xattn_Wo))
    w = np.asarray(L0_attn_in_proj_w)

    def blocks(rows):
        return rows.reshape(-1, GB, P, KC, P).transpose(0, 4, 1, 3, 2)

    a["wg"] = blocks(w[:inter])
    a["wx"] = blocks(w[inter:2 * inter])
    a["wbc"] = blocks(w[2 * inter:2 * inter + 2 * NG * P])
    a["wdt"] = by_partition(w[2 * inter + 2 * NG * P:].T)
    a["wout"] = np.asarray(L0_attn_out_proj_w).reshape(DM, NG, GB, P).transpose(1, 3, 2, 0)
    cols = np.zeros((P, NG + 2, GB, NPAR), f)
    order = list(range(NG, NG + 2)) + list(range(NG))
    cols[..., 0:TAPS] = np.asarray(L0_attn_conv_w).reshape(NG + 2, GB, P, TAPS).transpose(2, 0, 1, 3)[:, order]
    cols[..., 4] = np.asarray(L0_attn_conv_b).reshape(NG + 2, GB, P).transpose(2, 0, 1)[:, order]
    cols[:, 2:, :, 5] = np.repeat(np.asarray(L0_attn_D), 64).reshape(NG, GB, P).transpose(2, 0, 1)
    cols[:, 2:, :, 6] = np.asarray(L0_attn_norm_w).reshape(NG, GB, P).transpose(2, 0, 1)
    a["par"] = cols.reshape(P, NG + 2, GB * NPAR)
    a["dtb"] = np.asarray(L0_attn_dt_bias).reshape(1, P)
    a["bgate"] = np.asarray(L0_ffn_b_gate).reshape(1, NE)
    a["wgate"] = by_partition(np.asarray(L0_ffn_W_gate))
    a["we"] = np.asarray(L0_ffn_W_e).reshape(NE, KC, P, DM).transpose(0, 2, 1, 3)
    a["be"] = np.asarray(L0_ffn_b_e).reshape(1, NE * DM)

    nc = bacc.Bacc("TRN2", target_bir_lowering=False, num_devices=1)
    arrays, d = {}, {}
    for name, v in a.items():
        v = np.ascontiguousarray(v)
        arrays[f"in_{name}"] = v
        d[name] = nc.dram_tensor(f"in_{name}", v.shape, mybir.dt.from_np(v.dtype), kind="ExternalInput").ap()
    d["out"] = nc.dram_tensor("out", (1, P, DM), F32, kind="ExternalOutput").ap().rearrange("a b c -> (a b) c")
    build(nc, d)
    r = run_bass_kernel_spmd(nc, [arrays], core_ids=[0])
    return r.results[0]["out"]
```

```python
from contextlib import ExitStack

import concourse.bass as bass
from concourse import mybir

F32 = mybir.dt.float32
BF16 = mybir.dt.bfloat16
ALU = mybir.AluOpType
ACT = mybir.ActivationFunctionType
AX = mybir.AxisListType

P = 128
DM = 512
KC = DM // P
SK = 2048
HD = 16
KVH = 8
REP = 4
NKB = SK // P
KCOLS, QCOLS = SK, REP * P
SLOTS = 3
PAIRS = [(0, 0), (0, 1), (0, 2), (1, 0), (1, 1), (2, 0)]
KROWS = HD * len(PAIRS)
MROWS = 2
WARM = 8
KQ_LOADS = 12 * 16
KQ_EARLY = 12 * 16
KQ_REST = 6 * 16
SCALE = float(HD) ** -0.5
QN = 2
SBANKS = (4, 5, 7)


def score_bank(s, b):
    return SBANKS[(b + 2 * s) % 3]
NG = 8
GH = 16
GB = 8
HB = GB // 2
TAPS = 4
PADW = P + TAPS - 1
GROUP = GB * P
NPAR = 8
DT_MIN, DT_MAX = 0.001, 100.0
CPARTS = 3
NE = 8
EPS = 1e-5

C_ID, C_TRI, C_A, C_COMB, C_LT, C_END = 0, 128, 256, 384, 416, 480


def build(nc, d):
    ctx = ExitStack()
    with ctx:
        def sb(name, shape, dt=F32):
            return ctx.enter_context(nc.sbuf_tensor(name, shape, dt))

        def sem(name):
            return ctx.enter_context(nc.semaphore(name))

        res = sb("res", [P, DM])
        xn = sb("xn", [P, DM])
        xT = sb("xT", [P, KC, P])
        cst = sb("cst", [P, C_END])
        identb = sb("identb", [P, P], BF16)
        warm = xT[:, 0:2].rearrange("p k n -> p (k n)").bitcast(BF16)
        par = sb("par", [P, NG + 2, GB * NPAR])
        par_v = par[:, :, :].rearrange("p n (b c) -> p n b c", c=NPAR)
        cpar = sb("cpar", [P, GB, NPAR])
        wdt = sb("wdt", [P, KC, P])
        wgate = sb("wgate", [P, KC, NE])
        dtb = sb("dtb", [P, P])
        bgate = sb("bgate", [P, NE])
        dt = sb("dt", [P, P])
        dA = sb("dA", [P, P])
        csl = sb("csl", [P, P], BF16)
        csr = sb("csr", [P, GH * P], BF16)
        sqs = sb("sqs", [P, P])
        small = sb("small", [P, 160])
        wx = sb("wx", [P, GB, KC, P])
        wg = sb("wg", [P, GB, KC, P])
        wo = sb("wo", [P, GB * DM])
        wc_v = wo[:, :].rearrange("p (b k f) -> p b k f", b=GB, k=KC)
        wo_v = wo[:, :].rearrange("p (b n) -> p b n", b=GB)
        ps = ctx.enter_context(nc.psum_tensor("ps", [P, 8, 512], F32))

        ident = cst[:, C_ID:C_ID + P]
        tri = cst[:, C_TRI:C_TRI + P]
        acoef = cst[:, C_A:C_A + P]
        comb = cst[:, C_COMB:C_COMB + 32]
        lower = cst[:, C_LT:C_LT + NE * NE].rearrange("p (e j) -> p e j", e=NE)

        stats = small[:, 0:6]
        mean = small[:, 6:7]
        mv2 = small[:, 6:8]
        vareps = small[:, 8:9]
        rstd = small[:, 9:10]
        neghalf = small[:, 10:11]
        ones1 = small[:, 11:12]
        gvar = small[:, 12:13]
        grstd = small[:, 13:14]
        mx = small[:, 16:24]
        nm = small[:, 24:28]
        mparts = small[:, 28:32].bitcast(BF16).rearrange("p (r c) -> p r c", c=2)
        rden = small[:, 32:64]
        lg = small[:, 64:72]
        rank = small[:, 72:80]
        wsel = small[:, 80:88]

        A = sb("arena_a", [P, 20480])
        B = sb("arena_b", [P, 14336])

        def carve(arena, sizes):
            at, out = 0, []
            for n in sizes:
                out.append(arena[:, at:at + n])
                at += n
            assert at <= arena.shape[1], (at, arena.shape)
            return out

        ctx_s, woa_s, pvs_s, pb_s = carve(A, [4 * KC * 512, KC * DM, KVH * 512, 8 * 512])
        ctxT = ctx_s.rearrange("p (t k n) -> p t k n", t=4, k=KC)
        woa = woa_s.rearrange("p (k n) -> p k n", k=KC)
        pvs = pvs_s.rearrange("p (h n) -> p h n", h=KVH)
        pb = pb_s.rearrange("p (b n) -> p b n", b=8)
        resid = pb_s[:, 0:KCOLS + QCOLS]
        we_s, be_s = carve(A, [NE * KC * DM, NE * DM])
        we = we_s.rearrange("p (e k n) -> p e k n", e=NE, k=KC)
        be = be_s.rearrange("p (e n) -> p e n", e=NE)

        (wq_s, wk_s, wv_s, sp_s, kq_s, va_s, vw_s) = carve(
            B, [KC * DM, KC * P, KC * P, 3 * (KCOLS + QCOLS) // 2, SLOTS * (KCOLS + QCOLS) // 2,
                NKB * P, SLOTS * NKB * 32])
        wq = wq_s.rearrange("p (k n) -> p k n", k=KC)
        wk = wk_s.rearrange("p (k n) -> p k n", k=KC)
        wv = wv_s.rearrange("p (k n) -> p k n", k=KC)
        parts = sp_s.bitcast(BF16).rearrange("p (c n) -> p c n", c=3)
        kq = kq_s.bitcast(BF16).rearrange("p (s n) -> p s n", s=SLOTS)
        vall = va_s.rearrange("p (b h c) -> p b h c", b=NKB, h=KVH)
        vw = vw_s.rearrange("p (s b c) -> p s b c", s=SLOTS, b=NKB)
        csb = wq_s[:, 0:2 * 512].rearrange("p (f n) -> p f n", f=2)
        otok = wq_s[:, 1024:1024 + DM]

        (pre_s, xs_s, xdt_s, em_s, sg_s, xd_s, yg_s, yw_s, bt_s, ct_s, cb_s) = carve(
            B, [GB * PADW, 1024, 1024, 2048, 1024, 1024, 1024, 1024, 1024, 1024, 1024])
        pre = pre_s.rearrange("p (b n) -> p b n", b=GB)
        xs = xs_s.rearrange("p (b n) -> p b n", b=GB)
        xdt = xdt_s.rearrange("p (h n) -> p h n", h=GH)
        em = em_s.rearrange("p (c h n) -> p c h n", c=4, h=4)
        sg = sg_s.rearrange("p (b n) -> p b n", b=GB)
        xd = xd_s.rearrange("p (b n) -> p b n", b=GB)
        yg = yg_s.rearrange("p (b n) -> p b n", b=GB)
        yw = yw_s.rearrange("p (b n) -> p b n", b=GB)
        bt = bt_s.rearrange("p (g n) -> p g n", g=NG)
        ct = ct_s.rearrange("p (g n) -> p g n", g=NG)
        cbm = cb_s.rearrange("p (g n) -> p g n", g=NG)
        z, nz, ez, ez1, lnz, dz, rz = (em_s[:, n * P:(n + 1) * P] for n in range(7))
        csres = em_s[:, 7 * P:8 * P]
        csparts = em_s[:, 8 * P:8 * P + CPARTS * P // 2].bitcast(BF16).rearrange("p (c n) -> p c n", c=CPARTS)
        te = xs_s.rearrange("p (b n) -> p b n", b=2)
        re_ = xdt_s.rearrange("p (b n) -> p b n", b=2)
        cmp1 = yg_s[:, 0:64].rearrange("p (e j) -> p e j", e=NE)
        cmp2 = yg_s[:, 64:128].rearrange("p (e j) -> p e j", e=NE)

        ld_x, ld_cst, ld_wq, ld_wk, ld_wv, ld_woa = map(sem, ["ld_x", "ld_cst", "ld_wq", "ld_wk", "ld_wv", "ld_woa"])
        ld_ctx = [sem(f"ld_ctx{t}") for t in range(4)]
        ld_par, ld_wdt, ld_wx, ld_wg, ld_wo, ld_we, ld_be = map(
            sem, ["ld_par", "ld_wdt", "ld_wx", "ld_wg", "ld_wo", "ld_we", "ld_be"])
        cs_stored, ld_cs, ld_csconst = sem("cs_stored"), sem("ld_cs"), sem("ld_csconst")
        ld_kq = [sem(f"ld_kq{s}") for s in range(SLOTS)]
        ld_kq_early, ld_ctx0 = sem("ld_kq_early"), [sem("ld_ctx0a"), sem("ld_ctx0b")]
        warm_set = sem("warm_set")
        stored = sem("stored")
        const_set, ident_set = sem("const_set"), sem("ident_set")
        ln_step, rstd_ready, xt_psum, xt_copied = map(sem, ["ln_step", "rstd_ready", "xt_psum", "xt_copied"])
        qk_psum, part1, residual, part2, part3 = map(sem, ["qk_psum", "part1", "residual", "part2", "part3"])
        v_psum, v_copied, vslot_ready = map(sem, ["v_psum", "v_copied", "vslot_ready"])
        row_scores, row_maxed, m_step, m_rows, m_copied = map(
            sem, ["row_scores", "row_maxed", "m_step", "m_rows", "m_copied"])
        scores, probs, pv_groups, pv_saved = map(sem, ["scores", "probs", "pv_groups", "pv_saved"])
        combined, comb_copied, otr, onorm, ot_psum, ot_copied, attn_psum, attn_added = map(
            sem, ["combined", "comb_copied", "otr", "onorm", "ot_psum", "ot_copied", "attn_psum", "attn_added"])
        dt_psum, dt_step, dt_act = map(sem, ["dt_psum", "dt_step", "dt_act"])
        proj_psum, pre_ready, tap_done, conv_step, silu_done, cpar_set = map(
            sem, ["proj_psum", "pre_ready", "tap_done", "conv_step", "silu_done", "cpar_set"])
        cb_psum, cb_ready, cs_psum, cs_step, seg_psum, clamped, decay_done, em_ready = map(
            sem, ["cb_psum", "cb_ready", "cs_psum", "cs_step", "seg_psum", "clamped", "decay_done", "em_ready"])
        xtok_psum, xdt_ready, xd_ready, gate_psum, sg_done, y_psum, u_done, yg_ready = map(
            sem, ["xtok_psum", "xdt_ready", "xd_ready", "gate_psum", "sg_done", "y_psum", "u_done", "yg_ready"])
        sq_done, sqs_ready, ss_psum, gvar_ready, grstd_ready, yw_ready, o_psum, o_added = map(
            sem, ["sq_done", "sqs_ready", "ss_psum", "gvar_ready", "grstd_ready", "yw_ready", "o_psum", "o_added"])
        lg_psum, gate_step, e_psum, t_ready, r_ready, e_added = map(
            sem, ["lg_psum", "gate_step", "e_psum", "t_ready", "r_ready", "e_added"])

        chunks = [(slice(512 * n, 512 * n + 512), n) for n in range(4)]
        chunks.insert(QN, (slice(KCOLS, KCOLS + QCOLS), 7))

        block = ctx.enter_context(nc.Block())

        @block.sync
        def _(sp):
            sp.dma_start(wk, d["wk"]).then_inc(ld_wk, 16)
            for n in range(2):
                sp.dma_start(ctxT[:, 0, 2 * n:2 * n + 2], d["ctx"][0][:, 2 * n:2 * n + 2]).then_inc(ld_ctx0[n], 16)
            sp.dma_start(res[:], d["x"]).then_inc(ld_x, 16)
            sp.dma_start(ctxT[:, 1], d["ctx"][1]).then_inc(ld_ctx[1], 16)
            sp.dma_start(cst[:], d["cst"]).then_inc(ld_cst, 16)
            sp.dma_start(wq, d["wq"]).then_inc(ld_wq, 16)
            for t in range(2, 4):
                sp.dma_start(ctxT[:, t], d["ctx"][t]).then_inc(ld_ctx[t], 16)
            sp.dma_start(wv, d["wv"]).then_inc(ld_wv, 16)

            def stack(i, cols, n, first, count, same, done):
                s = i % SLOTS
                rows = slice(HD * i, HD * i + HD)
                for c in range(count):
                    part = first if same else first + c
                    sp.dma_start(kq[HD * (n + c):HD * (n + c + 1), s, cols],
                                 parts[rows, part, cols]).then_inc(done, 16)

            def stack_q(i, done):
                for n, count in ((0, 3), (3, 2), (5, 1)):
                    stack(i, slice(KCOLS, KCOLS + QCOLS), n, 0, count, same=False, done=done)

            def stack_k(i, done, cols=slice(0, KCOLS)):
                for n, part in ((0, 0), (3, 1), (5, 2)):
                    stack(i, cols, n, part, 3 - part, same=True, done=done)

            sp.wait_ge(part1, QN)
            sp.wait_ge(part2, QN)
            sp.wait_ge(part3, QN)
            stack_k(0, ld_kq_early, slice(0, KCOLS // 2))
            sp.wait_ge(part1, QN + 1)
            sp.wait_ge(part2, QN + 1)
            sp.wait_ge(part3, QN + 1)
            stack_q(0, ld_kq_early)
            sp.wait_ge(part1, 5)
            sp.wait_ge(part2, 5)
            sp.wait_ge(part3, 5)
            stack_k(0, ld_kq[0], slice(KCOLS // 2, KCOLS))
            for i in range(1, SLOTS):
                stack_q(i, ld_kq[i])
                stack_k(i, ld_kq[i])
            sp.dma_start(par[:], d["par"]).then_inc(ld_par, 16)
            sp.dma_start(dtb[:], d["dtb"].to_broadcast([P, P])).then_inc(ld_par, 16)
            sp.dma_start(bgate[:], d["bgate"].to_broadcast([P, NE])).then_inc(ld_par, 16)
            sp.dma_start(woa, d["woa"]).then_inc(ld_woa, 16)
            sp.dma_start(wdt[:], d["wdt"]).then_inc(ld_wdt, 16)
            sp.dma_start(wgate[:], d["wgate"]).then_inc(ld_wdt, 16)
            sp.dma_start(csl[:], d["csl"]).then_inc(ld_csconst, 16)
            sp.dma_start(csr[:], d["csr"]).then_inc(ld_csconst, 16)
            sp.dma_start(wg[:], d["wbc"][0]).then_inc(ld_wg, 16)
            for i in range(SLOTS, KVH):
                sp.wait_ge(scores, NKB * (i - 2))
                stack_q(i, ld_kq[i % SLOTS])
                stack_k(i, ld_kq[i % SLOTS])
                if i == SLOTS:
                    sp.dma_start(wc_v, d["wbc"][1]).then_inc(ld_wo, 16)
                if i == SLOTS + 1:
                    sp.dma_start(wx[:], d["wx"][0]).then_inc(ld_wx, 16)
            sp.wait_ge(proj_psum, 2)
            sp.dma_start(wg[:], d["wg"][0]).then_inc(ld_wg, 16)

            def stack_cs(g):
                sp.dma_start(csl[CPARTS:CPARTS + GH * CPARTS, :],
                             d["cs"][bass.ds(g * GH, GH)].rearrange("h c n -> (h c) n")).then_inc(ld_cs, 16)
                sp.dma_start(csr[0:CPARTS, :].rearrange("c (h n) -> c h n", h=GH),
                             d["cs"][bass.ds(g * GH, GH)].rearrange("h c n -> c h n")).then_inc(ld_cs, 16)

            sp.wait_ge(cs_step, 4)
            sp.dma_start(d["cs"], csparts).then_inc(cs_stored, 16)
            sp.wait_ge(cs_stored, 16)
            sp.wait_ge(ld_csconst, 32)
            stack_cs(0)
            sp.wait_ge(proj_psum, 4)
            sp.dma_start(wo_v, d["wout"][0]).then_inc(ld_wo, 16)
            sp.dma_start(be_s, d["be"].to_broadcast([P, NE * DM])).then_inc(ld_be, 16)

            def load_expert(e):
                sp.dma_start(we[:, bass.ds(e, 1)].rearrange("p o k n -> p (o k) n"),
                             d["we"][bass.ds(e, 1)].rearrange("o p k n -> (o p) k n")).then_inc(ld_we, 16)

            def reload(g, first=False, last=False):
                if not last:
                    sp.wait_ge(proj_psum, g * 2 + 6)
                    sp.dma_start(wx[:], d["wx"][bass.ds(g + 1, 1)].rearrange("o p b k f -> (o p) b k f")
                                 ).then_inc(ld_wx, 16)
                load_expert(g)
                if not first:
                    sp.wait_ge(o_psum, g)
                    sp.dma_start(wo_v, d["wout"][bass.ds(g, 1)].rearrange("o p b n -> (o p) b n")
                                 ).then_inc(ld_wo, 16)
                if not last:
                    sp.wait_ge(seg_psum, g * 4 + 4)
                    stack_cs(g + 1)
                    sp.wait_ge(gate_psum, g * 2 + 2)
                    sp.dma_start(wg[:], d["wg"][bass.ds(g + 1, 1)].rearrange("o p b k f -> (o p) b k f")
                                 ).then_inc(ld_wg, 16)

            reload(0, first=True)
            with sp.Fori(1, NG - 1) as g:
                reload(g)
            reload(NG - 1, last=True)
            sp.wait_ge(e_added, NE)
            sp.dma_start(d["out"], res[:]).then_inc(stored, 16)
            sp.wait_ge(stored, 16)

        @block.gpsimd
        def _(pool):
            fills = [(neghalf, -0.5), (ones1, 1.0), (vw[:, :, :, HD:32], 1.0)]
            fills += [(kq[KROWS:KROWS + MROWS, s, 0:KCOLS], 1.0) for s in range(SLOTS)]
            def rstd_of(n):
                pool.wait_ge(ln_step, n * 4 + 3)
                pool.tensor_tensor(rstd, vareps, neghalf, ALU.pow).then_inc(rstd_ready, 1)

            for n, (what, value) in enumerate(fills):
                if n:
                    pool.wait_ge(const_set, n)
                if n == 1:
                    rstd_of(0)
                pool.memset(what, value).then_inc(const_set, 1)

            def v_slot(i, s):
                pool.tensor_copy(vw[:, s, :, 0:HD],
vall[:, :, i, :]).then_inc(vslot_ready, 1)

            pool.wait_ge(v_copied, 4)
            for i in range(SLOTS):
                v_slot(i, i)
            for i in range(SLOTS, KVH):
                pool.wait_ge(pv_groups, 4 * (i - SLOTS) + 4)
                v_slot(i, i % SLOTS)
            rstd_of(1)

            def conv_params(n):
                pool.tensor_copy(cpar[:], par[:, bass.ds(n, 1), :].rearrange("p o (b c) -> p (o b) c", c=NPAR)
                                 ).then_inc(cpar_set, 1)

            pool.wait_ge(ld_par, 48)
            def skip_term(g, first=False):
                pool.wait_ge(silu_done, g * 2 + 6)
                if not first:
                    pool.wait_ge(sqs_ready, g)
                dcol = par[:, bass.ds(g + 2, 1), :].rearrange("p o (b c) -> p (o b) c", c=NPAR)[:, :, 5:6]
                pool.tensor_tensor(xd, xs, dcol.to_broadcast([P, GB, P]), ALU.mult).then_inc(xd_ready, 1)

            def norm_weight(g, first=False):
                if not first:
                    pool.wait_ge(o_psum, g)
                for h in range(2):
                    pool.wait_ge(yg_ready, g * 2 + h + 1)
                    wcol = par[:, bass.ds(g + 2, 1), HB * NPAR * h:HB * NPAR * (h + 1)].rearrange(
                        "p o (b c) -> p (o b) c", c=NPAR)[:, :, 6:7]
                    at = slice(HB * h, HB * h + HB)
                    pool.tensor_tensor(yw[:, at], yg[:, at], wcol.to_broadcast([P, HB, P]),
                                       ALU.mult).then_inc(yw_ready, 1)

            def group_rstd(g):
                pool.wait_ge(gvar_ready, g + 1)
                pool.tensor_tensor(grstd, gvar, neghalf, ALU.pow).then_inc(grstd_ready, 1)

            def group(g, first=False, last=False):
                if not first:
                    norm_weight(g - 1, first=isinstance(g, int) and g == 1)
                if not first:
                    group_rstd(g - 1)
                skip_term(g, first)
                if not last:
                    if not first:
                        pool.wait_ge(conv_step, g * 24 + 72)
                    conv_params(g + 3)

            group(0, first=True)
            group(1)
            with pool.Fori(2, NG - 1) as g:
                group(g)
            group(NG - 1, last=True)
            norm_weight(NG - 1)
            group_rstd(NG - 1)
            rstd_of(2)

        @block.scalar
        def _(act):
            def second_part(n):
                act.wait_ge(residual, n + 1)
                act.activation(parts[:, 1, chunks[n][0]], resid[:, chunks[n][0]], ACT.Copy).then_inc(part2, 1)

            for n in range(5):
                act.wait_ge(qk_psum, n + 1)
                act.activation(parts[:, 0, chunks[n][0]], ps[:, chunks[n][1], :], ACT.Copy).then_inc(part1, 1)
                second_part(n)
            for t in range(4):
                act.wait_ge(v_psum, t + 1)
                act.activation(vall[:, t * 4:t * 4 + 4], ps[:, 4 + t % 2, :].rearrange(
                    "p (b h c) -> p b h c", b=4, h=KVH), ACT.Copy).then_inc(v_copied, 1)

            def take_maxima(i, s):
                act.wait_ge(m_rows, i + 1)
                act.activation(kq[KROWS:KROWS + MROWS, s, KCOLS:],
                               ps[KROWS:KROWS + MROWS, score_bank((s + 2) % SLOTS, NKB), :], ACT.Copy).then_inc(m_copied, 1)

            def save_pv(i):
                act.wait_ge(pv_groups, i * 4 + 4)
                act.activation(pvs[:, bass.ds(i, 1)].rearrange("p o n -> p (o n)"), ps[:, 6, :],
                               ACT.Copy).then_inc(pv_saved, 1)

            def attend(i, s, first=False, last=False):
                for b in range(NKB):
                    if b == 2 and not first:
                        save_pv(i - 1)
                    if b == NKB - 1 and not last:
                        take_maxima(i + 1, (s + 1) % SLOTS)
                    act.wait_ge(scores, i * NKB + b + 1)
                    if not first or b >= 8:
                        act.wait_ge(pv_groups, i * 4 + b // 4 - 1)
                    act.activation(pb[:, b % 8], ps[:, score_bank(s, b), :], ACT.Exp, scale=SCALE).then_inc(probs, 1)

            take_maxima(0, 0)
            attend(0, 0, first=True)
            with act.Fori(0, 2) as t:
                for u in range(3):
                    attend(t * 3 + (1 + u), (1 + u) % SLOTS)
            attend(KVH - 1, (KVH - 1) % SLOTS, last=True)
            save_pv(KVH - 1)

            act.wait_ge(dt_step, 2)
            act.activation(ez, nz, ACT.Exp).then_inc(dt_act, 1)
            act.wait_ge(dt_step, 3)
            act.activation(lnz, ez1, ACT.Ln).then_inc(dt_act, 1)

            def take(n, h, banks, cp, free=None):
                act.wait_ge(proj_psum, n * 2 + h + 1)
                if free is not None:
                    act.wait_ge(conv_step, free)
                act.activation(pre[:, HB * h:HB * h + HB, TAPS - 1:],
                               ps[:, banks + h, :].rearrange("p (b n) -> p b n", b=HB),
                               ACT.Copy).then_inc(pre_ready, 1)
                for b in range(HB):
                    act.activation(xs[:, HB * h + b], ps[:, banks + h, P * b:P * b + P], ACT.Identity,
                                   scale=cp[:, HB * h + b, 3:4], bias=cp[:, HB * h + b, 4:5]).then_inc(tap_done, 1)

            def silu(n, h, to):
                act.wait_ge(conv_step, n * 24 + 12 * h + 12)
                act.activation(to[:, HB * h:HB * h + HB], xs[:, HB * h:HB * h + HB],
                               ACT.Silu).then_inc(silu_done, 1)

            act.wait_ge(ld_par, 48)
            for h in range(2):
                take(0, h, 0, par_v[:, 0])
            for n, to, banks in ((1, bt, 2), (2, ct, 0)):
                for h in range(2):
                    silu(n - 1, h, to)
                    act.wait_ge(silu_done, 2 * n + h - 1)
                    take(n, h, banks, par_v[:, n], free=24 * (n - 1) + 12 * (h + 1))

            def square(g):
                act.wait_ge(yg_ready, g * 2 + 2)
                act.activation(xd, yg, ACT.Square).then_inc(sq_done, 1)

            def clamps(g, first=False):
                if first:
                    act.wait_ge(cs_stored, 16)
                else:
                    act.wait_ge(y_psum, g * 2)
                for c in range(4):
                    act.wait_ge(seg_psum, g * 4 + c + 1)
                    act.activation(em[:, c], ps[:, 4 + c % 2, :].rearrange("p (h n) -> p h n", h=4),
                                   ACT.Relu, scale=-1.0).then_inc(clamped, 1)

            def decays(g):
                for c in range(4):
                    act.wait_ge(clamped, g * 4 + c + 1)
                    act.activation(em[:, c], em[:, c], ACT.Exp, scale=-1.0).then_inc(decay_done, 1)

            def group(g, first=False):
                if not first:
                    square(g - 1)
                    act.wait_ge(cpar_set, g)
                    act.wait_ge(xtok_psum, g * 2)
                    act.wait_ge(xd_ready, g)
                    for h in range(2):
                        take(g + 2, h, 0, cpar, free=g * 24 + (24 + 12 * (h + 1)))
                else:
                    clamps(g, first=True)
                for h in range(2):
                    silu(g + 2, h, xs)
                if not first:
                    clamps(g)
                decays(g)
                if not first:
                    act.wait_ge(yg_ready, g * 2)
                for h in range(2):
                    act.wait_ge(gate_psum, g * 2 + h + 1)
                    act.activation(sg[:, HB * h:HB * h + HB],
                                   ps[:, 2 + h, :].rearrange("p (b n) -> p b n", b=HB),
                                   ACT.Silu).then_inc(sg_done, 1)

            group(0, first=True)
            with act.Fori(1, NG) as g:
                group(g)
            square(NG - 1)

            def expert(e, s, first=False):
                act.wait_ge(t_ready, e + 1)
                if not first:
                    act.wait_ge(e_added, e - 1)
                act.activation(re_[:, s], te[:, s], ACT.Relu,
                               scale=wsel[:, bass.ds(e, 1)]).then_inc(r_ready, 1)

            act.wait_ge(gate_step, 7)
            for e in (0, 1):
                expert(e, e, first=True)
            with act.Fori(1, NE // 2) as pair:
                for u in range(2):
                    expert(pair * 2 + u, u)

        @block.vector
        def _(dve):
            def layer_norm(n):
                dve.bn_stats(stats, res[:]).then_inc(ln_step, 1)
                dve.wait_ge(ln_step, n * 4 + 1)
                dve.bn_aggr(mv2, stats).then_inc(ln_step, 1)
                dve.wait_ge(ln_step, n * 4 + 2)
                dve.tensor_scalar(vareps, small[:, 7:8], EPS, None, ALU.add).then_inc(ln_step, 1)
                dve.wait_ge(rstd_ready, n + 1)
                dve.tensor_scalar(xn[:], res[:], mean, rstd, ALU.subtract, ALU.mult).then_inc(ln_step, 1)

            def take_transposed(n, bank):
                dve.wait_ge(xt_psum, n + 1)
                dve.tensor_copy(xT[:], ps[:, bank, :].rearrange("p (k n) -> p k n", k=KC)).then_inc(xt_copied, 1)

            dve.memset(xT[:, 0:2], 0.0).then_inc(warm_set, 1)
            dve.wait_ge(ld_x, 16)
            layer_norm(0)
            dve.wait_ge(ld_cst, 16)
            dve.tensor_copy(identb[:], ident).then_inc(ident_set, 1)
            take_transposed(0, 6)

            def third_part(n):
                dve.wait_ge(part2, n + 1)
                dve.tensor_tensor(parts[:, 2, chunks[n][0]], resid[:, chunks[n][0]], parts[:, 1, chunks[n][0]],
                                  ALU.subtract).then_inc(part3, 1)

            for n in range(5):
                dve.wait_ge(part1, n + 1)
                dve.tensor_tensor(resid[:, chunks[n][0]], ps[:, chunks[n][1], :], parts[:, 0, chunks[n][0]],
                                  ALU.subtract).then_inc(residual, 1)
                third_part(n)

            def maxima(i, first=False):
                for c in range(8):
                    dve.wait_ge(row_scores, i * 8 + c + 1)
                    dve.tensor_reduce(mx[:, c:c + 1], ps[:, 2 * (c % 2):2 * (c % 2) + 2, :],
                                      AX.XY, ALU.max).then_inc(row_maxed, 1)
                dve.wait_ge(row_maxed, i * 8 + 8)
                dve.tensor_reduce(nm, mx.rearrange("p (c r) -> p r c", c=2), AX.X, ALU.max,
                                  negate=True).then_inc(m_step, 1)
                dve.wait_ge(m_step, i * 3 + 1)
                if not first:
                    dve.wait_ge(m_rows, i)
                dve.tensor_copy(mparts[:, :, 0], nm).then_inc(m_step, 1)
                dve.wait_ge(m_step, i * 3 + 2)
                dve.tensor_tensor(mparts[:, :, 1], nm, mparts[:, :, 0], ALU.subtract).then_inc(m_step, 1)

            maxima(0, first=True)
            with dve.Fori(1, KVH) as i:
                maxima(i)

            for f in range(2):
                dve.wait_ge(combined, f + 1)
                dve.tensor_copy(csb[:, f], ps[:, (0, 3)[f], :]).then_inc(comb_copied, 1)
                dve.wait_ge(otr, f + 1)
                by_head = ps[:, 2, :].rearrange("p (r j c) -> p r j c", r=REP, j=4)
                dve.reciprocal(rden[:, 16 * f:16 * f + 16].rearrange("p (n o) -> p n o", o=1),
                               ps[:, 2, :].rearrange("p (n c) -> p n c", c=32)[:, :, HD:HD + 1]
                               ).then_inc(onorm, 1)
                dve.wait_ge(onorm, 2 * f + 1)
                dve.tensor_tensor(
                    otok[:, 256 * f:256 * f + 256].rearrange("p (j r c) -> p r j c", j=4, r=REP),
                    by_head[:, :, :, 0:HD],
                    rden[:, 16 * f:16 * f + 16].rearrange("p (r j) -> p r j", r=REP).unsqueeze(3)
                    .to_broadcast([P, REP, 4, HD]), ALU.mult).then_inc(onorm, 1)
                dve.wait_ge(ot_psum, f + 1)
                dve.tensor_copy(xT[:, 2 * f:2 * f + 2], ps[:, 0, 256 * f:256 * f + 256].rearrange(
                    "p (k n) -> p k n", k=2)).then_inc(ot_copied, 1)
            dve.wait_ge(attn_psum, 1)
            dve.tensor_tensor(res[:], ps[:, 1, :], res[:], ALU.add).then_inc(attn_added, 1)
            dve.wait_ge(attn_added, 1)
            layer_norm(1)
            dve.memset(pre[:, :, 0:TAPS - 1], 0.0)
            take_transposed(1, 6)

            def step(n):
                dve.wait_ge(dt_step, n)

            dve.wait_ge(dt_psum, 1)
            dve.wait_ge(ld_par, 48)
            dve.tensor_tensor(z, ps[:, 7, 0:P], dtb[:], ALU.add).then_inc(dt_step, 1)
            step(1)
            dve.scalar_tensor_tensor(nz, z, -1.0, z, ALU.mult, ALU.min).then_inc(dt_step, 1)
            dve.wait_ge(dt_act, 1)
            dve.tensor_scalar(ez1, ez, 1.0, None, ALU.add).then_inc(dt_step, 1)
            step(3)
            dve.tensor_scalar(dz, ez1, -1.0, 1e-30, ALU.add, ALU.max).then_inc(dt_step, 1)
            step(4)
            dve.reciprocal(rz, dz).then_inc(dt_step, 1)
            step(5)
            dve.tensor_tensor(rz, rz, ez, ALU.mult).then_inc(dt_step, 1)
            step(6)
            dve.wait_ge(dt_act, 2)
            dve.tensor_tensor(rz, rz, lnz, ALU.mult).then_inc(dt_step, 1)
            step(7)
            dve.scalar_tensor_tensor(dt[:], z, 0.0, rz, ALU.max, ALU.add).then_inc(dt_step, 1)
            step(8)
            dve.tensor_scalar(dt[:], dt[:], DT_MIN, DT_MAX, ALU.max, ALU.min).then_inc(dt_step, 1)
            step(9)
            dve.tensor_tensor(dA[:], dt[:], acoef, ALU.mult).then_inc(dt_step, 1)

            def conv(n, h, cp):
                dve.wait_ge(pre_ready, n * 2 + h + 1)
                for k in reversed(range(TAPS - 1)):
                    for j in range(HB):
                        b = HB * h + j
                        if k == TAPS - 2:
                            dve.wait_ge(tap_done, n * 8 + (b + 1))
                        else:
                            dve.wait_ge(conv_step, n * 24 + (12 * h + HB * (TAPS - 3 - k) + j + 1))
                        dve.scalar_tensor_tensor(xs[:, b], pre[:, b, k:k + P], cp[:, b, k:k + 1],
                                                 xs[:, b], ALU.mult, ALU.add).then_inc(conv_step, 1)

            def cs_parts():
                dve.wait_ge(cs_psum, 1)
                dve.tensor_copy(csparts[:, 0], ps[:, 7, P:2 * P]).then_inc(cs_step, 1)
                dve.wait_ge(cs_step, 1)
                dve.tensor_tensor(csres, ps[:, 7, P:2 * P], csparts[:, 0], ALU.subtract).then_inc(cs_step, 1)
                dve.wait_ge(cs_step, 2)
                dve.tensor_copy(csparts[:, 1], csres).then_inc(cs_step, 1)
                dve.wait_ge(cs_step, 3)
                dve.tensor_tensor(csparts[:, 2], csres, csparts[:, 1], ALU.subtract).then_inc(cs_step, 1)

            for h in range(2):
                conv(0, h, par_v[:, 0])
            cs_parts()
            for h in range(2):
                conv(1, h, par_v[:, 1])

            def masked_cb():
                for h in range(2):
                    dve.wait_ge(cb_psum, h + 1)
                    dve.tensor_tensor(cbm[:, 4 * h:4 * h + 4],
                                      ps[:, 6 + h, :].rearrange("p (g n) -> p g n", g=4),
                                      tri.unsqueeze(1).to_broadcast([P, 4, P]), ALU.mult).then_inc(cb_ready, 1)

            def gated(g, first=False):
                dve.wait_ge(xd_ready, g + 1)
                if not first:
                    dve.wait_ge(sq_done, g)
                    dve.wait_ge(yw_ready, g * 2)
                dve.wait_ge(sg_done, g * 2 + 2)
                for h in range(2):
                    at = slice(HB * h, HB * h + HB)
                    dve.wait_ge(y_psum, g * 2 + h + 1)
                    dve.tensor_tensor(yg[:, at], ps[:, 4 + h, :].rearrange("p (b n) -> p b n", b=HB),
                                      xd[:, at], ALU.add).then_inc(u_done, 1)
                    dve.wait_ge(u_done, g * 2 + h + 1)
                    dve.tensor_tensor(yg[:, at], yg[:, at], sg[:, at], ALU.mult).then_inc(yg_ready, 1)

            def sum_squares(g, first=False):
                dve.wait_ge(sq_done, g + 1)
                if not first:
                    dve.wait_ge(ss_psum, g)
                dve.tensor_reduce(sqs[:], xd.rearrange("p b n -> p n b"), AX.X, ALU.add).then_inc(sqs_ready, 1)

            def group_variance(g):
                dve.wait_ge(ss_psum, g + 1)
                dve.tensor_scalar(gvar, ps[:, 7, 0:1], 1.0 / GROUP, EPS, ALU.mult, ALU.add).then_inc(gvar_ready, 1)

            def add_group(g):
                dve.wait_ge(grstd_ready, g + 1)
                dve.wait_ge(o_psum, g + 1)
                dve.scalar_tensor_tensor(res[:], ps[:, 6, :], grstd, res[:], ALU.mult, ALU.add).then_inc(o_added, 1)

            def times_dt(g):
                for h in range(2):
                    dve.wait_ge(xtok_psum, g * 2 + h + 1)
                    dve.tensor_tensor(
                        xdt[:, GB * h:GB * h + GB], ps[:, h, :].rearrange("p (n c) -> p n c", n=8),
                        dt[:, bass.ds(g * GH + GB * h, GB)].unsqueeze(2).to_broadcast([P, GB, 64]),
                        ALU.mult).then_inc(xdt_ready, 1)

            def group(g, first=False, second=False):
                if not first:
                    gated(g - 1, first=second)
                    sum_squares(g - 1, first=second)
                if first:
                    conv(2, 0, par_v[:, 2])
                    masked_cb()
                    conv(2, 1, par_v[:, 2])
                    dve.wait_ge(cb_ready, 2)
                else:
                    for h in range(2):
                        conv(g + 2, h, cpar)
                    group_variance(g - 1)
                if first:
                    times_dt(g)
                for c in range(4):
                    dve.wait_ge(decay_done, g * 4 + c + 1)
                    dve.tensor_tensor(em[:, c], em[:, c], cbm[:, bass.ds(g, 1)].to_broadcast([P, 4, P]),
                                      ALU.mult).then_inc(em_ready, 1)
                if not first:
                    add_group(g - 1)
                    times_dt(g)

            group(0, first=True)
            group(1, second=True)
            with dve.Fori(2, NG) as g:
                group(g)
            gated(NG - 1)
            sum_squares(NG - 1)
            group_variance(NG - 1)
            add_group(NG - 1)
            dve.wait_ge(o_added, NG)

            layer_norm(2)
            take_transposed(2, 6)
            dve.wait_ge(lg_psum, 1)
            dve.tensor_tensor(lg, ps[:, 7, 0:NE], bgate[:], ALU.add).then_inc(gate_step, 1)
            dve.wait_ge(gate_step, 1)
            lg_j = lg.unsqueeze(1).to_broadcast([P, NE, NE])
            lg_e = lg.unsqueeze(2).to_broadcast([P, NE, NE])
            dve.tensor_tensor(cmp1, lg_j, lg_e, ALU.is_gt).then_inc(gate_step, 1)
            dve.tensor_tensor(cmp2, lg_j, lg_e, ALU.is_equal).then_inc(gate_step, 1)
            dve.wait_ge(gate_step, 3)
            dve.tensor_tensor(cmp2, cmp2, lower, ALU.mult).then_inc(gate_step, 1)
            dve.wait_ge(gate_step, 4)
            dve.tensor_tensor(cmp1, cmp1, cmp2, ALU.add).then_inc(gate_step, 1)
            dve.wait_ge(gate_step, 5)
            dve.tensor_reduce(rank, cmp1, AX.X, ALU.add).then_inc(gate_step, 1)
            dve.wait_ge(gate_step, 6)
            dve.tensor_scalar(wsel, rank, 1.5, 0.5, ALU.is_lt, ALU.mult).then_inc(gate_step, 1)

            def add_bias(e, s, first=False):
                dve.wait_ge(e_psum, e + 1)
                if not first:
                    dve.wait_ge(r_ready, e - 1)
                dve.tensor_tensor(te[:, s], ps[:, s, :], be[:, bass.ds(e, 1)].rearrange("p o n -> p (o n)"),
                                  ALU.add).then_inc(t_ready, 1)

            def add_expert(e, s, first=False):
                dve.wait_ge(r_ready, e + 1)
                if not first:
                    dve.wait_ge(e_added, e)
                dve.tensor_tensor(res[:], res[:], re_[:, s], ALU.add).then_inc(e_added, 1)

            dve.wait_ge(ld_be, 16)
            add_bias(0, 0, first=True)
            add_bias(1, 1, first=True)
            add_expert(0, 0, first=True)
            with dve.Fori(1, NE // 2) as pair:
                for u in range(2):
                    add_bias(pair * 2 + u, u)
                    add_expert(pair * 2 + u - 1, 1 - u)
            add_expert(NE - 1, 1)

        @block.tensor
        def _(pe):
            def transpose_xn(n, src, bank):
                for k in range(KC):
                    last = pe.transpose(ps[:, bank, P * k:P * k + P], src[:, P * k:P * k + P], ident)
                last.then_inc(xt_psum, 1)

            def project_k(t):
                if t:
                    pe.wait_ge(ld_ctx[t], 16)
                for k in range(KC):
                    if t == 0 and k % 2 == 0:
                        pe.wait_ge(ld_ctx0[k // 2], 16)
                    last = pe.matmul(ps[:, t, :], wk[:, k], ctxT[:, t, k], start=k == 0, stop=k == KC - 1)
                last.then_inc(qk_psum, 1)

            pe.wait_ge(warm_set, 1)
            for n in range(WARM):
                pe.matmul(ps[:, 6, :], warm[:, 0:P], warm[:, 0:512], start=True, stop=True)
            pe.wait_ge(ld_wk, 16)
            for t in range(QN):
                project_k(t)
            pe.wait_ge(ld_cst, 16)
            pe.wait_ge(ln_step, 4)
            transpose_xn(0, xn, 6)
            pe.wait_ge(xt_copied, 1)
            pe.wait_ge(ld_wq, 16)
            for r in range(REP):
                for k in range(KC):
                    last = pe.matmul(ps[:, 7, P * r:P * r + P], wq[:, k, P * r:P * r + P], xT[:, k],
                                     start=k == 0, stop=k == KC - 1)
            last.then_inc(qk_psum, 1)
            for t in range(QN, 4):
                project_k(t)
            pe.wait_ge(ld_wv, 16)

            def project_v(t, b):
                if b == 0 and t >= 2:
                    pe.wait_ge(v_copied, t - 1)
                for k in range(KC):
                    last = pe.matmul(ps[:, 4 + t % 2, P * b:P * b + P], ctxT[:, t, k, P * b:P * b + P],
                                     wv[:, k], start=k == 0, stop=k == KC - 1)
                if b == 3:
                    last.then_inc(v_psum, 1)

            def rows(i, s, c, first=False):
                if not first:
                    pe.wait_ge(row_maxed, i * 8 + c - 1)
                r, half = c % REP, c // REP
                for j in range(2):
                    at = 1024 * half + 512 * j
                    last = pe.matmul(ps[:, 2 * (c % 2) + j, :], kq[0:KROWS, s, KCOLS + P * r:KCOLS + P * r + P],
                                     kq[0:KROWS, s, at:at + 512], start=True, stop=True)
                last.then_inc(row_scores, 1)

            def maxima_to_rows(i, s):
                pe.wait_ge(m_step, i * 3 + 3)
                bank = score_bank(s, NKB)
                for r in range(REP):
                    last = pe.matmul(ps[KROWS:KROWS + MROWS, bank, P * r:P * r + P], mparts[:, r], identb[:],
                                     start=True, stop=True, tile_position=(0, KROWS))
                last.then_inc(m_rows, 1)

            def columns(i, s, b, first=False):
                if b == 0:
                    pe.wait_ge(m_copied, i + 1)
                if b == 2:
                    pass
                elif not (first and b < 3):
                    pe.wait_ge(probs, i * NKB + (b - 2 if b > 2 else b - 1))
                pe.matmul(ps[:, score_bank(s, b), :], kq[0:KROWS + MROWS, s, P * b:P * b + P],
                          kq[0:KROWS + MROWS, s, KCOLS:], start=True, stop=True).then_inc(scores, 1)

            def product(i, s, grp):
                pe.wait_ge(probs, i * NKB + 4 * grp + 4)
                if grp == 0:
                    pe.wait_ge(vslot_ready, i + 1)
                for j in range(4):
                    last = pe.matmul(ps[32 * j:32 * j + 32, 6, :], vw[:, s, 4 * grp + j], pb[:, (4 * grp + j) % 8],
                                     start=grp == 0, stop=grp == 3, tile_position=(0, 32 * j))
                last.then_inc(pv_groups, 1)

            def quarter(i, s, grp, turns=None, ahead=True, maxima=True):
                n, c = (i + 1, 2 * grp + 2) if grp < 3 else (i + 2, 0)
                slot = (s + (1 if grp < 3 else 2)) % SLOTS
                first = isinstance(i, int) and i == 0
                columns(i, s, 4 * grp, first)
                columns(i, s, 4 * grp + 1, first)
                if ahead:
                    if grp == 3:
                        pe.wait_ge(ld_kq[slot], turns)
                    rows(n, slot, c)
                if grp in (1, 2):
                    product(i, s, grp - 1)
                elif grp == 0 and not first:
                    product(i - 1, (s + 2) % SLOTS, 3)
                columns(i, s, 4 * grp + 2, first)
                if ahead and grp < 3:
                    rows(n, slot, c + 1)
                columns(i, s, 4 * grp + 3, first)
                if grp == 3 and maxima:
                    pe.wait_ge(probs, i * NKB + 14)
                    maxima_to_rows(i + 1, s)
                if grp == 3:
                    product(i, s, 2)
                if ahead and grp == 3:
                    rows(n, slot, c + 1)

            pe.wait_ge(const_set, 6)
            n_v = 0
            for c in range(8):
                while n_v < (3 + c if c < 4 else 4 + c):
                    project_v(n_v // 4, n_v % 4)
                    n_v += 1
                if c == 0:
                    pe.wait_ge(ld_kq_early, KQ_EARLY)
                    pe.wait_ge(residual, 5)
                if c == 4:
                    pe.wait_ge(ld_kq[0], KQ_REST)
                rows(0, 0, c, first=c < 2)
            for n in range(n_v, NKB):
                project_v(n // 4, n % 4)
            pe.wait_ge(ld_kq[1], KQ_LOADS)
            rows(1, 1, 0)
            rows(1, 1, 1)
            pe.wait_ge(ident_set, 1)
            pe.wait_ge(v_copied, 4)
            maxima_to_rows(0, SLOTS - 1)
            quarter(0, 0, 0)
            with pe.Fori(0, 2) as t:
                for u in range(3):
                    turns = t * KQ_LOADS + (KQ_LOADS * ((u + 2) // SLOTS + 1)
                                            - (KQ_LOADS - KQ_REST) * ((u + 2) % SLOTS == 0))
                    for grp in range(1, 4):
                        quarter(t * 3 + u, u, grp, turns)
                    quarter(t * 3 + (u + 1), (u + 1) % SLOTS, 0)
            for grp in range(1, 4):
                quarter(KVH - 2, (KVH - 2) % SLOTS, grp, ahead=grp < 3)

            def combine(f, js):
                pe.wait_ge(pv_saved, 4 * f + js[-1] + 1)
                for j in js:
                    last = pe.matmul(ps[32 * j:32 * j + 32, (0, 3)[f], :], comb, pvs[:, 4 * f + j],
                                     start=True, stop=True, tile_position=(0, 32 * j))
                if js[-1] == 3:
                    last.then_inc(combined, 1)

            def by_token(f):
                pe.wait_ge(comb_copied, f + 1)
                if f:
                    pe.wait_ge(onorm, 2)
                for r in range(REP):
                    last = pe.transpose(ps[:, 2, P * r:P * r + P], csb[:, f, P * r:P * r + P], ident)
                last.then_inc(otr, 1)

            def by_feature(f):
                pe.wait_ge(onorm, 2 * f + 2)
                for k in (2 * f, 2 * f + 1):
                    last = pe.transpose(ps[:, 0, P * k:P * k + P], otok[:, P * k:P * k + P], ident)
                last.then_inc(ot_psum, 1)

            def project_attention(f):
                pe.wait_ge(ot_copied, f + 1)
                for k in (2 * f, 2 * f + 1):
                    last = pe.matmul(ps[:, 1, :], xT[:, k], woa[:, k], start=k == 0, stop=k == KC - 1)
                if f:
                    last.then_inc(attn_psum, 1)

            i, s = KVH - 1, (KVH - 1) % SLOTS
            pe.wait_ge(row_maxed, 8 * KVH)
            quarter(i, s, 0, ahead=False)
            combine(0, (0, 1, 2, 3))
            quarter(i, s, 1, ahead=False)
            combine(1, (0, 1, 2))
            by_token(0)
            quarter(i, s, 2, ahead=False)
            by_feature(0)
            quarter(i, s, 3, ahead=False, maxima=False)
            product(i, s, 3)
            pe.wait_ge(ld_woa, 16)
            project_attention(0)
            combine(1, (3,))
            by_token(1)
            by_feature(1)
            project_attention(1)

            pe.wait_ge(ln_step, 8)
            transpose_xn(1, xn, 6)
            pe.wait_ge(xt_copied, 2)
            pe.wait_ge(ld_wdt, 32)
            for k in range(KC):
                last = pe.matmul(ps[:, 7, 0:P], xT[:, k], wdt[:, k], start=k == 0, stop=k == KC - 1)
            last.then_inc(dt_psum, 1)

            def project(w, banks, done, halves=(0, 1)):
                for b in range(HB * halves[0], HB * halves[-1] + HB):
                    for k in range(KC):
                        last = pe.matmul(ps[:, banks + b // HB, P * (b % HB):P * (b % HB) + P],
                                         w[:, b, k], xT[:, k], start=k == 0, stop=k == KC - 1)
                    if b % HB == HB - 1:
                        last.then_inc(done, 1)

            pe.wait_ge(ld_wg, 16)
            project(wg, 0, proj_psum)
            pe.wait_ge(dt_step, 10)
            pe.matmul(ps[:, 7, P:2 * P], dA[:], tri, start=True, stop=True).then_inc(cs_psum, 1)
            pe.wait_ge(ld_wo, 16)
            project(wc_v, 2, proj_psum)

            def out_proj(g, first=False):
                pe.wait_ge(ld_wo, g * 16 + 32)
                if not first:
                    pe.wait_ge(o_added, g)
                for b in range(GB):
                    if b % HB == 0:
                        pe.wait_ge(yw_ready, g * 2 + b // HB + 1)
                    last = pe.matmul(ps[:, 6, :], yw[:, b], wo_v[:, b], start=b == 0, stop=b == GB - 1)
                last.then_inc(o_psum, 1)
                pe.wait_ge(sqs_ready, g + 1)
                pe.matmul(ps[:, 7, 0:1], sqs[:], ones1, start=True, stop=True).then_inc(ss_psum, 1)

            def segments(g, cs):
                for c in cs:
                    if c >= 2:
                        pe.wait_ge(clamped, g * 4 + c - 1)
                    pe.matmul(ps[:, 4 + c % 2, :], csl[:], csr[:, 512 * c:512 * c + 512],
                              start=True, stop=True).then_inc(seg_psum, 1)

            def gates(g, first=False, halves=(0, 1)):
                pe.wait_ge(ld_wg, g * 16 + 32)
                if first:
                    pe.wait_ge(tap_done, 16)
                else:
                    pe.wait_ge(sg_done, g * 2)
                project(wg, 2, gate_psum, halves)

            def group(g, first=False, second=False):
                pe.wait_ge(ld_wx, g * 16 + 16)
                if first:
                    pe.wait_ge(tap_done, 8)
                else:
                    pe.wait_ge(xdt_ready, g * 2)
                project(wx, 0, proj_psum)
                if first:
                    pe.wait_ge(ld_cs, 32)
                    segments(g, (0, 1))
                    pe.wait_ge(silu_done, 4)
                    for n in range(NG):
                        last = pe.matmul(ps[:, 6 + n // 4, P * (n % 4):P * (n % 4) + P], bt[:, n], ct[:, n],
                                         start=True, stop=True)
                        if n % 4 == 3:
                            last.then_inc(cb_psum, 1)
                    segments(g, (2, 3))
                    gates(g, first=True, halves=(0,))
                else:
                    out_proj(g - 1, first=second)
                    pe.wait_ge(u_done, g * 2)
                    pe.wait_ge(ld_cs, g * 32 + 32)
                    segments(g, (0, 1))
                for h in range(2):
                    pe.wait_ge(silu_done, g * 2 + h + 5)
                    for b in range(HB):
                        last = pe.transpose(ps[:, h, P * b:P * b + P], xs[:, HB * h + b], ident)
                    last.then_inc(xtok_psum, 1)
                if first:
                    gates(g, first=True, halves=(1,))
                else:
                    segments(g, (2, 3))
                    gates(g)
                pe.wait_ge(em_ready, g * 4 + 4)
                pe.wait_ge(xdt_ready, g * 2 + 2)
                for b in range(GB):
                    for o in range(2):
                        h = 2 * b + o
                        last = pe.matmul(ps[64 * o:64 * o + 64, 4 + b // HB, P * (b % HB):P * (b % HB) + P],
                                         xdt[:, h], em[:, h // 4, h % 4], start=True, stop=True,
                                         tile_position=(0, 64 * o))
                    if b % HB == HB - 1:
                        last.then_inc(y_psum, 1)

            group(0, first=True)
            group(1, second=True)
            with pe.Fori(2, NG) as g:
                group(g)
            out_proj(NG - 1)

            pe.wait_ge(ln_step, 12)
            transpose_xn(2, xn, 6)
            pe.wait_ge(xt_copied, 3)
            for k in range(KC):
                last = pe.matmul(ps[:, 7, 0:NE], xT[:, k], wgate[:, k], start=k == 0, stop=k == KC - 1)
            last.then_inc(lg_psum, 1)
            pe.wait_ge(ld_we, 16 * NE)

            def expert(e, s, first=False):
                if not first:
                    pe.wait_ge(t_ready, e - 1)
                for k in range(KC):
                    last = pe.matmul(ps[:, s, :], xT[:, k], we[:, bass.ds(e, 1), k].rearrange("p o n -> p (o n)"),
                                     start=k == 0, stop=k == KC - 1)
                last.then_inc(e_psum, 1)

            for e in (0, 1):
                expert(e, e, first=True)
            with pe.Fori(1, NE // 2) as pair:
                for u in range(2):
                    expert(pair * 2 + u, u)


def kernel(x, ctx_4096, L0_xattn_Wq, L0_xattn_Wk, L0_xattn_Wv, L0_xattn_Wo, L0_attn_in_proj_w,
           L0_attn_conv_w, L0_attn_conv_b, L0_attn_dt_bias, L0_attn_D, L0_attn_norm_w,
           L0_attn_out_proj_w, L0_ffn_W_gate, L0_ffn_b_gate, L0_ffn_W_e, L0_ffn_b_e):
    import numpy as np
    from ml_dtypes import bfloat16 as bf16
    import concourse.bacc as bacc
    from concourse.bass_utils import run_bass_kernel_spmd

    f = np.float32
    inter = NG * GROUP
    a = {}

    def by_partition(w):
        return w.reshape(KC, P, w.shape[-1]).transpose(1, 0, 2)

    i = np.arange(P)
    cst = np.zeros((P, C_END), f)
    cst[:, C_ID:C_ID + P] = np.eye(P)
    cst[:, C_TRI:C_TRI + P] = i[:, None] <= i[None, :]
    cst[:, C_A:C_A + P] = -(i[None, :] + 1.0)
    cst[:, C_COMB:C_COMB + HD] = (i % 32)[:, None] == np.arange(HD)[None, :]
    cst[:, C_COMB + HD:C_COMB + 32] = ((i % 32) == HD)[:, None]
    cst[:, C_LT:C_END] = np.tril(np.ones((NE, NE)), -1).ravel()[None, :]
    a["cst"] = cst

    csl = np.zeros((P, P), bf16)
    csl[:CPARTS] = 1
    csr = np.zeros((P, GH, P), bf16)
    for h in range(GH):
        csr[CPARTS * (h + 1):CPARTS * (h + 2), h] = -1
    a["csl"], a["csr"] = csl, csr.reshape(P, GH * P)

    a["x"] = np.asarray(x).reshape(P, DM)
    a["ctx"] = np.asarray(ctx_4096).reshape(4, 512, KC, P).transpose(0, 3, 2, 1)
    wq = np.asarray(L0_xattn_Wq).reshape(DM, KVH, REP, HD).transpose(0, 2, 1, 3).reshape(DM, DM)
    a["wq"] = by_partition(wq)
    a["wk"] = by_partition(np.asarray(L0_xattn_Wk))
    a["wv"] = by_partition(np.asarray(L0_xattn_Wv))
    a["woa"] = by_partition(np.asarray(L0_xattn_Wo))
    w = np.asarray(L0_attn_in_proj_w)

    def blocks(rows):
        return rows.reshape(-1, GB, P, KC, P).transpose(0, 4, 1, 3, 2)

    a["wg"] = blocks(w[:inter])
    a["wx"] = blocks(w[inter:2 * inter])
    a["wbc"] = blocks(w[2 * inter:2 * inter + 2 * NG * P])
    a["wdt"] = by_partition(w[2 * inter + 2 * NG * P:].T)
    a["wout"] = np.asarray(L0_attn_out_proj_w).reshape(DM, NG, GB, P).transpose(1, 3, 2, 0)
    cols = np.zeros((P, NG + 2, GB, NPAR), f)
    order = list(range(NG, NG + 2)) + list(range(NG))
    cols[..., 0:TAPS] = np.asarray(L0_attn_conv_w).reshape(NG + 2, GB, P, TAPS).transpose(2, 0, 1, 3)[:, order]
    cols[..., 4] = np.asarray(L0_attn_conv_b).reshape(NG + 2, GB, P).transpose(2, 0, 1)[:, order]
    cols[:, 2:, :, 5] = np.repeat(np.asarray(L0_attn_D), 64).reshape(NG, GB, P).transpose(2, 0, 1)
    cols[:, 2:, :, 6] = np.asarray(L0_attn_norm_w).reshape(NG, GB, P).transpose(2, 0, 1)
    a["par"] = cols.reshape(P, NG + 2, GB * NPAR)
    a["dtb"] = np.asarray(L0_attn_dt_bias).reshape(1, P)
    a["bgate"] = np.asarray(L0_ffn_b_gate).reshape(1, NE)
    a["wgate"] = by_partition(np.asarray(L0_ffn_W_gate))
    a["we"] = np.asarray(L0_ffn_W_e).reshape(NE, KC, P, DM).transpose(0, 2, 1, 3)
    a["be"] = np.asarray(L0_ffn_b_e).reshape(1, NE * DM)

    nc = bacc.Bacc("TRN2", target_bir_lowering=False, num_devices=1)
    arrays, d = {}, {}
    for name, v in a.items():
        v = np.ascontiguousarray(v)
        arrays[f"in_{name}"] = v
        d[name] = nc.dram_tensor(f"in_{name}", v.shape, mybir.dt.from_np(v.dtype), kind="ExternalInput").ap()
    d["cs"] = nc.dram_tensor("cs_parts", (P, CPARTS, P), BF16).ap()
    d["out"] = nc.dram_tensor("out", (1, P, DM), F32, kind="ExternalOutput").ap().rearrange("a b c -> (a b) c")
    build(nc, d)
    r = run_bass_kernel_spmd(nc, [arrays], core_ids=[0])
    return r.results[0]["out"]
```

```python
from contextlib import ExitStack

import concourse.bass as bass
from concourse import mybir

F32 = mybir.dt.float32
BF16 = mybir.dt.bfloat16
F32R = mybir.dt.float32r
ALU = mybir.AluOpType
ACT = mybir.ActivationFunctionType
AX = mybir.AxisListType

P = 128
DM = 512
KC = DM // P
SK = 2048
HD = 16
KVH = 8
REP = 4
NKB = SK // P
KCOLS, QCOLS = SK, REP * P
SLOTS = 3
PAIRS = [(0, 0), (0, 1), (0, 2), (1, 0), (1, 1), (2, 0)]
KROWS = HD * len(PAIRS)
MROWS = 2
WARM = 9
KQ_LOADS = 12 * 16
KQ_EARLY = 12 * 16
KQ_REST = 6 * 16
SCALE = float(HD) ** -0.5
QN = 2
SBANKS = (4, 5, 7)


def score_bank(s, b):
    return SBANKS[(b + 2 * s) % 3]
NG = 8
GH = 16
GB = 8
HB = GB // 2
TAPS = 4
PADW = P + TAPS - 1
GROUP = GB * P
NPAR = 8
DT_MIN, DT_MAX = 0.001, 100.0
CPARTS = 3
NE = 8
EPS = 1e-5

C_ID, C_TRI, C_A, C_COMB, C_LT, C_END = 0, 128, 256, 384, 416, 480


def build(nc, d):
    ctx = ExitStack()
    with ctx:
        def sb(name, shape, dt=F32):
            return ctx.enter_context(nc.sbuf_tensor(name, shape, dt))

        def sem(name):
            return ctx.enter_context(nc.semaphore(name))

        res = sb("res", [P, DM])
        xn = sb("xn", [P, DM])
        xT = sb("xT", [P, KC, P])
        cst = sb("cst", [P, C_END])
        identb = sb("identb", [P, P], BF16)
        warm = xT[:, 0:2].rearrange("p k n -> p (k n)").bitcast(BF16)
        par = sb("par", [P, NG + 2, GB * NPAR])
        par_v = par[:, :, :].rearrange("p n (b c) -> p n b c", c=NPAR)
        cpar = sb("cpar", [P, GB, NPAR])
        wdt = sb("wdt", [P, KC, P])
        wgate = sb("wgate", [P, KC, NE])
        dtb = sb("dtb", [P, P])
        bgate = sb("bgate", [P, NE])
        dt = sb("dt", [P, P])
        dA = sb("dA", [P, P])
        csl = sb("csl", [P, P], BF16)
        csr = sb("csr", [P, GH * P], BF16)
        sqs = sb("sqs", [P, P])
        small = sb("small", [P, 160])
        wx = sb("wx", [P, GB, KC, P])
        ps = ctx.enter_context(nc.psum_tensor("ps", [P, 8, 512], F32))

        ident = cst[:, C_ID:C_ID + P]
        tri = cst[:, C_TRI:C_TRI + P]
        acoef = cst[:, C_A:C_A + P]
        comb = cst[:, C_COMB:C_COMB + 32]
        lower = cst[:, C_LT:C_LT + NE * NE].rearrange("p (e j) -> p e j", e=NE)

        stats = small[:, 0:6]
        mean = small[:, 6:7]
        mv2 = small[:, 6:8]
        vareps = small[:, 8:9]
        rstd = small[:, 9:10]
        neghalf = small[:, 10:11]
        ones1 = small[:, 11:12]
        gvar = small[:, 12:13]
        grstd = small[:, 13:14]
        mx = small[:, 16:24]
        nm = small[:, 24:28]
        mparts = small[:, 28:32].bitcast(BF16).rearrange("p (r c) -> p r c", c=2)
        rden = small[:, 32:64]
        lg = small[:, 64:72]
        rank = small[:, 72:80]
        wsel = small[:, 80:88]

        B = sb("arena_b", [P, 12288])
        with ExitStack() as early:
            wo = early.enter_context(nc.sbuf_tensor("wo", [P, GB * DM], F32))
            bc = early.enter_context(nc.sbuf_tensor("bc", [P, 2048], F32))
            wg = early.enter_context(nc.sbuf_tensor("wg", [P, GB, KC, P], F32))
            A = early.enter_context(nc.sbuf_tensor("arena_a", [P, 20480], F32))
        wo_l = sb("wo_low", [P, GB, DM], F32R)
        yw_h = sb("yw_high", [P, GB, P], F32R)
        yw_l = sb("yw_low", [P, GB, P], F32R)
        we_h = sb("we_high", [P, 2, KC, DM], F32R)
        wo_h = sb("wo_high", [P, GB, DM], F32R)
        with ExitStack() as early:
            we = early.enter_context(nc.sbuf_tensor("we", [P, NE, KC, DM], F32))
        we_l = sb("we_low", [P, NE, KC, DM], F32R)
        x_h, x_l = yw_h[:, 0:KC], yw_l[:, 0:KC]
        wc_v = wo[:, :].rearrange("p (b k f) -> p b k f", b=GB, k=KC)
        wo_v = wo[:, :].rearrange("p (b n) -> p b n", b=GB)

        def carve(arena, sizes):
            at, out = 0, []
            for n in sizes:
                out.append(arena[:, at:at + n])
                at += n
            assert at <= arena.shape[1], (at, arena.shape)
            return out

        woa_s, pvs_s, pb_s, _, ctx_s = carve(A, [KC * DM, KVH * 512, 8 * 512, 2048, 4 * KC * 512])
        ctxT = ctx_s.rearrange("p (t k n) -> p t k n", t=4, k=KC)
        woa = woa_s.rearrange("p (k n) -> p k n", k=KC)
        pvs = pvs_s.rearrange("p (h n) -> p h n", h=KVH)
        pb = pb_s.rearrange("p (b n) -> p b n", b=8)
        resid = pb_s[:, 0:KCOLS + QCOLS]
        be_s = wx[:, :].rearrange("p b k f -> p (b k f)")
        be = be_s.rearrange("p (e n) -> p e n", e=NE)

        (wq_s, wk_s, wv_s, sp_s, kq_s, vw_s) = carve(
            B, [KC * DM, KC * P, KC * P, 3 * (KCOLS + QCOLS) // 2, SLOTS * (KCOLS + QCOLS) // 2,
                SLOTS * NKB * 32])
        wq = wq_s.rearrange("p (k n) -> p k n", k=KC)
        wk = wk_s.rearrange("p (k n) -> p k n", k=KC)
        wv = wv_s.rearrange("p (k n) -> p k n", k=KC)
        parts = sp_s.bitcast(BF16).rearrange("p (c n) -> p c n", c=3)
        kq = kq_s.bitcast(BF16).rearrange("p (s n) -> p s n", s=SLOTS)
        vall = bc[:, :].rearrange("p (b h c) -> p b h c", b=NKB, h=KVH)
        vw = vw_s.rearrange("p (s b c) -> p s b c", s=SLOTS, b=NKB)
        csb = wq_s[:, 0:2 * 512].rearrange("p (f n) -> p f n", f=2)
        otok = wq_s[:, 1024:1024 + DM]

        (pre_s, xs_s, xdt_s, em_s, sg_s, xd_s, yg_s, yw_s, cb_s) = carve(
            B, [GB * PADW, 1024, 1024, 2048, 1024, 1024, 1024, 1024, 1024])
        pre = pre_s.rearrange("p (b n) -> p b n", b=GB)
        xs = xs_s.rearrange("p (b n) -> p b n", b=GB)
        xdt = xdt_s.rearrange("p (h n) -> p h n", h=GH)
        em = em_s.rearrange("p (c h n) -> p c h n", c=4, h=4)
        sg = sg_s.rearrange("p (b n) -> p b n", b=GB)
        xd = xd_s.rearrange("p (b n) -> p b n", b=GB)
        yg = yg_s.rearrange("p (b n) -> p b n", b=GB)
        yw = yw_s.rearrange("p (b n) -> p b n", b=GB)
        bt = bc[:, 0:1024].rearrange("p (g n) -> p g n", g=NG)
        ct = bc[:, 1024:2048].rearrange("p (g n) -> p g n", g=NG)
        cbm = cb_s.rearrange("p (g n) -> p g n", g=NG)
        z, nz, ez, ez1, lnz, dz, rz = (em_s[:, n * P:(n + 1) * P] for n in range(7))
        csres = em_s[:, 7 * P:8 * P]
        csparts = em_s[:, 8 * P:8 * P + CPARTS * P // 2].bitcast(BF16).rearrange("p (c n) -> p c n", c=CPARTS)
        te = xs_s.rearrange("p (b n) -> p b n", b=2)
        re_ = xdt_s.rearrange("p (b n) -> p b n", b=2)
        cmp1 = yg_s[:, 0:64].rearrange("p (e j) -> p e j", e=NE)
        cmp2 = yg_s[:, 64:128].rearrange("p (e j) -> p e j", e=NE)

        ld_x, ld_cst, ld_wq, ld_wk, ld_wv, ld_woa = map(sem, ["ld_x", "ld_cst", "ld_wq", "ld_wk", "ld_wv", "ld_woa"])
        ld_ctx = [sem(f"ld_ctx{t}") for t in range(4)]
        ld_par, ld_wdt, ld_wx, ld_wg, ld_wo, ld_we, ld_be = map(
            sem, ["ld_par", "ld_wdt", "ld_wx", "ld_wg", "ld_wo", "ld_we", "ld_be"])
        cs_stored, ld_cs, ld_csconst = sem("cs_stored"), sem("ld_cs"), sem("ld_csconst")
        ld_kq = [sem(f"ld_kq{s}") for s in range(SLOTS)]
        ld_kq_early, ld_ctx0 = sem("ld_kq_early"), [sem("ld_ctx0a"), sem("ld_ctx0b")]
        warm_set = sem("warm_set")
        stored = sem("stored")
        const_set, ident_set = sem("const_set"), sem("ident_set")
        ln_step, rstd_ready, xt_psum, xt_copied = map(sem, ["ln_step", "rstd_ready", "xt_psum", "xt_copied"])
        qk_psum, part1, residual, part2, part3 = map(sem, ["qk_psum", "part1", "residual", "part2", "part3"])
        v_psum, v_copied, vslot_ready = map(sem, ["v_psum", "v_copied", "vslot_ready"])
        row_scores, row_maxed, m_step, m_rows, m_copied = map(
            sem, ["row_scores", "row_maxed", "m_step", "m_rows", "m_copied"])
        scores, probs, pv_groups, pv_saved = map(sem, ["scores", "probs", "pv_groups", "pv_saved"])
        combined, comb_copied, otr, onorm, ot_psum, ot_copied, attn_psum, attn_added = map(
            sem, ["combined", "comb_copied", "otr", "onorm", "ot_psum", "ot_copied", "attn_psum", "attn_added"])
        dt_psum, dt_step, dt_act = map(sem, ["dt_psum", "dt_step", "dt_act"])
        proj_psum, pre_ready, tap_done, conv_step, silu_done, cpar_set = map(
            sem, ["proj_psum", "pre_ready", "tap_done", "conv_step", "silu_done", "cpar_set"])
        cb_psum, cb_ready, cs_psum, cs_step, seg_psum, clamped, decay_done, em_ready = map(
            sem, ["cb_psum", "cb_ready", "cs_psum", "cs_step", "seg_psum", "clamped", "decay_done", "em_ready"])
        xtok_psum, xdt_ready, xd_ready, gate_psum, sg_done, y_psum, u_done, yg_ready = map(
            sem, ["xtok_psum", "xdt_ready", "xd_ready", "gate_psum", "sg_done", "y_psum", "u_done", "yg_ready"])
        sq_done, sqs_ready, ss_psum, gvar_ready, grstd_ready, yw_ready, o_psum, o_added = map(
            sem, ["sq_done", "sqs_ready", "ss_psum", "gvar_ready", "grstd_ready", "yw_ready", "o_psum", "o_added"])
        woh_ready, wol_ready, ywh_ready, ywl_ready = map(sem, ["woh_ready", "wol_ready", "ywh_ready", "ywl_ready"])
        wol3_ready = sem("wol3_ready")
        weh_ready, wel_pool, wel_dve, x_parts = map(sem, ["weh_ready", "wel_pool", "wel_dve", "x_parts"])
        lg_psum, gate_step, e_psum, t_ready, r_ready, e_added = map(
            sem, ["lg_psum", "gate_step", "e_psum", "t_ready", "r_ready", "e_added"])

        halves = (slice(0, DM // 2), slice(DM // 2, DM))

        chunks = [(slice(512 * n, 512 * n + 512), n) for n in range(4)]
        chunks.insert(QN, (slice(KCOLS, KCOLS + QCOLS), 7))

        block = ctx.enter_context(nc.Block())

        @block.sync
        def _(sp):
            sp.dma_start(wk, d["wk"]).then_inc(ld_wk, 16)
            for n in range(2):
                sp.dma_start(ctxT[:, 0, 2 * n:2 * n + 2], d["ctx"][0][:, 2 * n:2 * n + 2]).then_inc(ld_ctx0[n], 16)
            sp.dma_start(res[:], d["x"]).then_inc(ld_x, 16)
            sp.dma_start(ctxT[:, 1], d["ctx"][1]).then_inc(ld_ctx[1], 16)
            sp.dma_start(cst[:], d["cst"]).then_inc(ld_cst, 16)
            sp.dma_start(wq, d["wq"]).then_inc(ld_wq, 16)
            for t in range(2, 4):
                sp.dma_start(ctxT[:, t], d["ctx"][t]).then_inc(ld_ctx[t], 16)
            sp.dma_start(wv, d["wv"]).then_inc(ld_wv, 16)

            def stack(i, cols, n, first, count, same, done):
                s = i % SLOTS
                rows = slice(HD * i, HD * i + HD)
                for c in range(count):
                    part = first if same else first + c
                    sp.dma_start(kq[HD * (n + c):HD * (n + c + 1), s, cols],
                                 parts[rows, part, cols]).then_inc(done, 16)

            def stack_q(i, done):
                for n, count in ((0, 3), (3, 2), (5, 1)):
                    stack(i, slice(KCOLS, KCOLS + QCOLS), n, 0, count, same=False, done=done)

            def stack_k(i, done, cols=slice(0, KCOLS)):
                for n, part in ((0, 0), (3, 1), (5, 2)):
                    stack(i, cols, n, part, 3 - part, same=True, done=done)

            sp.wait_ge(part1, QN)
            sp.wait_ge(part2, QN)
            sp.wait_ge(part3, QN)
            stack_k(0, ld_kq_early, slice(0, KCOLS // 2))
            sp.wait_ge(part1, QN + 1)
            sp.wait_ge(part2, QN + 1)
            sp.wait_ge(part3, QN + 1)
            stack_q(0, ld_kq_early)
            sp.wait_ge(part1, 5)
            sp.wait_ge(part2, 5)
            sp.wait_ge(part3, 5)
            stack_k(0, ld_kq[0], slice(KCOLS // 2, KCOLS))
            for i in range(1, SLOTS):
                stack_q(i, ld_kq[i])
                stack_k(i, ld_kq[i])
            sp.dma_start(par[:], d["par"]).then_inc(ld_par, 16)
            sp.dma_start(dtb[:], d["dtb"].to_broadcast([P, P])).then_inc(ld_par, 16)
            sp.dma_start(bgate[:], d["bgate"].to_broadcast([P, NE])).then_inc(ld_par, 16)
            sp.dma_start(woa, d["woa"]).then_inc(ld_woa, 16)
            sp.dma_start(wdt[:], d["wdt"]).then_inc(ld_wdt, 16)
            sp.dma_start(wgate[:], d["wgate"]).then_inc(ld_wdt, 16)
            sp.dma_start(csl[:], d["csl"]).then_inc(ld_csconst, 16)
            sp.dma_start(csr[:], d["csr"]).then_inc(ld_csconst, 16)
            sp.dma_start(wg[:], d["wbc"][0]).then_inc(ld_wg, 16)
            def load_expert(e):
                sp.dma_start(we[:, e], d["we"][e]).then_inc(ld_we, 16)

            sp.wait_ge(v_psum, 4)
            for i in range(SLOTS, KVH):
                sp.wait_ge(scores, NKB * (i - 2))
                stack_q(i, ld_kq[i % SLOTS])
                stack_k(i, ld_kq[i % SLOTS])
                if i == SLOTS:
                    sp.dma_start(wc_v, d["wbc"][1]).then_inc(ld_wo, 16)
                if i == SLOTS + 1:
                    sp.dma_start(wx[:], d["wx"][0]).then_inc(ld_wx, 16)
                load_expert(i)
            sp.wait_ge(proj_psum, 2)
            sp.dma_start(wg[:], d["wg"][0]).then_inc(ld_wg, 16)

            def stack_cs(g):
                sp.dma_start(csl[CPARTS:CPARTS + GH * CPARTS, :],
                             d["cs"][bass.ds(g * GH, GH)].rearrange("h c n -> (h c) n")).then_inc(ld_cs, 16)
                sp.dma_start(csr[0:CPARTS, :].rearrange("c (h n) -> c h n", h=GH),
                             d["cs"][bass.ds(g * GH, GH)].rearrange("h c n -> c h n")).then_inc(ld_cs, 16)

            sp.wait_ge(cs_step, 4)
            sp.dma_start(d["cs"], csparts).then_inc(cs_stored, 16)
            sp.wait_ge(cs_stored, 16)
            sp.wait_ge(ld_csconst, 32)
            stack_cs(0)
            sp.wait_ge(proj_psum, 4)
            sp.dma_start(wo_v, d["wout"][0]).then_inc(ld_wo, 16)

            def reload(g, first=False, last=False):
                if not last:
                    sp.wait_ge(proj_psum, g * 2 + 6)
                    sp.dma_start(wx[:], d["wx"][bass.ds(g + 1, 1)].rearrange("o p b k f -> (o p) b k f")
                                 ).then_inc(ld_wx, 16)
                if not first:
                    sp.wait_ge(o_psum, g)
                    sp.dma_start(wo_v, d["wout"][bass.ds(g, 1)].rearrange("o p b n -> (o p) b n")
                                 ).then_inc(ld_wo, 16)
                if not last:
                    sp.wait_ge(seg_psum, g * 4 + 4)
                    stack_cs(g + 1)
                    sp.wait_ge(gate_psum, g * 2 + 2)
                    sp.dma_start(wg[:], d["wg"][bass.ds(g + 1, 1)].rearrange("o p b k f -> (o p) b k f")
                                 ).then_inc(ld_wg, 16)

            load_expert(0)
            reload(0, first=True)
            with sp.Fori(1, NG - 1) as g:
                reload(g)
            reload(NG - 1, last=True)
            for e in range(1, SLOTS):
                load_expert(e)
            sp.wait_ge(proj_psum, NG * 2 + 4)
            sp.dma_start(be_s, d["be"].to_broadcast([P, NE * DM])).then_inc(ld_be, 16)
            for h in range(2):
                sp.wait_ge(e_added, NE + h)
                sp.dma_start(d["out"][:, DM // 2 * h:DM // 2 * (h + 1)],
                             res[:, DM // 2 * h:DM // 2 * (h + 1)]).then_inc(stored, 16)
            sp.wait_ge(stored, 32)

        @block.gpsimd
        def _(pool):
            fills = [(neghalf, -0.5), (ones1, 1.0), (vw[:, :, :, HD:32], 1.0)]
            fills += [(kq[KROWS:KROWS + MROWS, s, 0:KCOLS], 1.0) for s in range(SLOTS)]
            def rstd_of(n):
                pool.wait_ge(ln_step, n * 4 + 3)
                pool.tensor_tensor(rstd, vareps, neghalf, ALU.pow).then_inc(rstd_ready, 1)

            for n, (what, value) in enumerate(fills):
                if n:
                    pool.wait_ge(const_set, n)
                if n == 1:
                    rstd_of(0)
                pool.memset(what, value).then_inc(const_set, 1)

            def v_slot(i, s):
                pool.tensor_copy(vw[:, s, :, 0:HD], vall[:, :, i, :]).then_inc(vslot_ready, 1)

            pool.wait_ge(v_copied, 4)
            for i in range(SLOTS):
                v_slot(i, i)
            for i in range(SLOTS, KVH):
                pool.wait_ge(pv_groups, 4 * (i - SLOTS) + 4)
                v_slot(i, i % SLOTS)
            rstd_of(1)

            def conv_params(n):
                pool.tensor_copy(cpar[:], par[:, bass.ds(n, 1), :].rearrange("p o (b c) -> p (o b) c", c=NPAR)
                                 ).then_inc(cpar_set, 1)

            pool.wait_ge(ld_par, 48)
            def skip_term(g, first=False):
                pool.wait_ge(silu_done, g * 2 + 6)
                if not first:
                    pool.wait_ge(sqs_ready, g)
                dcol = par[:, bass.ds(g + 2, 1), :].rearrange("p o (b c) -> p (o b) c", c=NPAR)[:, :, 5:6]
                pool.tensor_tensor(xd, xs, dcol.to_broadcast([P, GB, P]), ALU.mult).then_inc(xd_ready, 1)

            def norm_weight(g, first=False):
                if not first:
                    pool.wait_ge(o_psum, g)
                for h in range(2):
                    pool.wait_ge(yg_ready, g * 2 + h + 1)
                    wcol = par[:, bass.ds(g + 2, 1), HB * NPAR * h:HB * NPAR * (h + 1)].rearrange(
                        "p o (b c) -> p (o b) c", c=NPAR)[:, :, 6:7]
                    at = slice(HB * h, HB * h + HB)
                    pool.tensor_tensor(yw[:, at], yg[:, at], wcol.to_broadcast([P, HB, P]),
                                       ALU.mult).then_inc(yw_ready, 1)

            def weights_low(g, q):
                pool.wait_ge(woh_ready, g * 4 + (q + 1))
                pool.tensor_tensor(wo_l[:, 2 * q:2 * q + 2], wo_v[:, 2 * q:2 * q + 2],
                                   wo_h[:, 2 * q:2 * q + 2], ALU.subtract).then_inc(wol_ready, 1)

            def group_rstd(g):
                pool.wait_ge(gvar_ready, g + 1)
                pool.tensor_tensor(grstd, gvar, neghalf, ALU.pow).then_inc(grstd_ready, 1)

            def group(g, first=False, last=False):
                if not first:
                    norm_weight(g - 1, first=isinstance(g, int) and g == 1)
                if not first:
                    weights_low(g - 1, 1)
                    weights_low(g - 1, 2)
                    group_rstd(g - 1)
                skip_term(g, first)
                if not last:
                    if not first:
                        pool.wait_ge(conv_step, g * 24 + 72)
                    conv_params(g + 3)
                if not last:
                    weights_low(g, 0)

            group(0, first=True)
            group(1)
            with pool.Fori(2, NG - 1) as g:
                group(g)
            group(NG - 1, last=True)
            norm_weight(NG - 1)
            for q in range(2):
                weights_low(NG - 1, q)
            group_rstd(NG - 1)
            rstd_of(2)

            def expert_low(e, s):
                pool.wait_ge(weh_ready, e * 2 + 1)
                pool.tensor_tensor(we_l[:, bass.ds(e, 1), 0:2].rearrange("p o k n -> p (o k) n"),
                                   we[:, bass.ds(e, 1), 0:2].rearrange("p o k n -> p (o k) n"),
                                   we_h[:, s, 0:2], ALU.subtract).then_inc(wel_pool, 1)

            for e in (0, 1):
                expert_low(e, e)
            with pool.Fori(1, NE // 2) as pair:
                for u in range(2):
                    expert_low(pair * 2 + u, u)

        @block.scalar
        def _(act):
            def second_part(n):
                act.wait_ge(residual, n + 1)
                act.activation(parts[:, 1, chunks[n][0]], resid[:, chunks[n][0]], ACT.Copy).then_inc(part2, 1)

            for n in range(5):
                act.wait_ge(qk_psum, n + 1)
                act.activation(parts[:, 0, chunks[n][0]], ps[:, chunks[n][1], :], ACT.Copy).then_inc(part1, 1)
                second_part(n)
            for t in range(4):
                act.wait_ge(v_psum, t + 1)
                act.activation(vall[:, t * 4:t * 4 + 4], ps[:, 4 + t % 2, :].rearrange(
                    "p (b h c) -> p b h c", b=4, h=KVH), ACT.Copy).then_inc(v_copied, 1)

            def take_maxima(i, s):
                act.wait_ge(m_rows, i + 1)
                act.activation(kq[KROWS:KROWS + MROWS, s, KCOLS:],
                               ps[KROWS:KROWS + MROWS, score_bank((s + 2) % SLOTS, NKB), :],
                               ACT.Copy).then_inc(m_copied, 1)

            def save_pv(i):
                act.wait_ge(pv_groups, i * 4 + 4)
                act.activation(pvs[:, bass.ds(i, 1)].rearrange("p o n -> p (o n)"), ps[:, 6, :],
                               ACT.Copy).then_inc(pv_saved, 1)

            def attend(i, s, first=False, last=False):
                for b in range(NKB):
                    if b == 2 and not first:
                        save_pv(i - 1)
                    if b == NKB - 1 and not last:
                        take_maxima(i + 1, (s + 1) % SLOTS)
                    act.wait_ge(scores, i * NKB + b + 1)
                    if not first or b >= 8:
                        act.wait_ge(pv_groups, i * 4 + b // 4 - 1)
                    act.activation(pb[:, b % 8], ps[:, score_bank(s, b), :], ACT.Exp, scale=SCALE).then_inc(probs, 1)

            take_maxima(0, 0)
            attend(0, 0, first=True)
            with act.Fori(0, 2) as t:
                for u in range(3):
                    attend(t * 3 + (1 + u), (1 + u) % SLOTS)
            attend(KVH - 1, (KVH - 1) % SLOTS, last=True)
            save_pv(KVH - 1)

            act.wait_ge(dt_step, 2)
            act.activation(ez, nz, ACT.Exp).then_inc(dt_act, 1)
            act.wait_ge(dt_step, 3)
            act.activation(lnz, ez1, ACT.Ln).then_inc(dt_act, 1)

            def take(n, h, banks, cp, free=None):
                act.wait_ge(proj_psum, n * 2 + h + 1)
                if free is not None:
                    act.wait_ge(conv_step, free)
                act.activation(pre[:, HB * h:HB * h + HB, TAPS - 1:],
                               ps[:, banks + h, :].rearrange("p (b n) -> p b n", b=HB),
                               ACT.Copy).then_inc(pre_ready, 1)
                for b in range(HB):
                    act.activation(xs[:, HB * h + b], ps[:, banks + h, P * b:P * b + P], ACT.Identity,
                                   scale=cp[:, HB * h + b, 3:4], bias=cp[:, HB * h + b, 4:5]).then_inc(tap_done, 1)

            def silu(n, h, to):
                act.wait_ge(conv_step, n * 24 + 12 * h + 12)
                act.activation(to[:, HB * h:HB * h + HB], xs[:, HB * h:HB * h + HB],
                               ACT.Silu).then_inc(silu_done, 1)

            act.wait_ge(ld_par, 48)
            for h in range(2):
                take(0, h, 0, par_v[:, 0])
            for n, to, banks in ((1, bt, 2), (2, ct, 0)):
                for h in range(2):
                    silu(n - 1, h, to)
                    act.wait_ge(silu_done, 2 * n + h - 1)
                    take(n, h, banks, par_v[:, n], free=24 * (n - 1) + 12 * (h + 1))

            def square(g):
                act.wait_ge(yg_ready, g * 2 + 2)
                act.activation(xd, yg, ACT.Square).then_inc(sq_done, 1)

            def weights_high(g, qs):
                act.wait_ge(ld_wo, g * 16 + 32)
                for q in qs:
                    act.activation(wo_h[:, 2 * q:2 * q + 2], wo_v[:, 2 * q:2 * q + 2],
                                   ACT.Copy).then_inc(woh_ready, 1)

            def operand_high(g):
                for h in range(2):
                    act.wait_ge(yw_ready, g * 2 + h + 1)
                    act.activation(yw_h[:, HB * h:HB * h + HB], yw[:, HB * h:HB * h + HB],
                                   ACT.Copy).then_inc(ywh_ready, 1)

            def clamps(g, cs, first=False):
                if first:
                    act.wait_ge(cs_stored, 16)
                else:
                    act.wait_ge(y_psum, g * 2)
                for c in cs:
                    act.wait_ge(seg_psum, g * 4 + c + 1)
                    act.activation(em[:, c], ps[:, 4 + c % 2, :].rearrange("p (h n) -> p h n", h=4),
                                   ACT.Relu, scale=-1.0).then_inc(clamped, 1)

            def decays(g):
                for c in range(4):
                    act.wait_ge(clamped, g * 4 + c + 1)
                    act.activation(em[:, c], em[:, c], ACT.Exp, scale=-1.0).then_inc(decay_done, 1)

            def group(g, first=False):
                if not first:
                    operand_high(g - 1)
                    square(g - 1)
                    act.wait_ge(cpar_set, g)
                    act.wait_ge(xtok_psum, g * 2)
                    act.wait_ge(xd_ready, g)
                    for h in range(2):
                        take(g + 2, h, 0, cpar, free=g * 24 + (24 + 12 * (h + 1)))
                        clamps(g, (2 * h, 2 * h + 1))
                else:
                    clamps(g, range(4), first=True)
                for h in range(2):
                    silu(g + 2, h, xs)
                decays(g)
                if not first:
                    act.wait_ge(yg_ready, g * 2)
                for h in range(2):
                    act.wait_ge(gate_psum, g * 2 + h + 1)
                    act.activation(sg[:, HB * h:HB * h + HB],
                                   ps[:, 2 + h, :].rearrange("p (b n) -> p b n", b=HB),
                                   ACT.Silu).then_inc(sg_done, 1)
                    if h == 0:
                        weights_high(g, (0,))
                weights_high(g, (1, 2, 3))

            group(0, first=True)
            with act.Fori(1, NG) as g:
                group(g)
            operand_high(NG - 1)
            square(NG - 1)

            def expert_high(e, s, first=False):
                if not first:
                    act.wait_ge(e_psum, e - 1)
                for h in range(2):
                    act.activation(we_h[:, s, 2 * h:2 * h + 2],
                                   we[:, bass.ds(e, 1), 2 * h:2 * h + 2].rearrange("p o k n -> p (o k) n"),
                                   ACT.Copy).then_inc(weh_ready, 1)

            act.wait_ge(ld_we, 16 * NE)
            act.wait_ge(gate_psum, 2 * NG)
            for e in (0, 1):
                expert_high(e, e, first=True)
            act.wait_ge(o_psum, NG)
            act.wait_ge(xt_psum, 3)
            act.activation(x_h, ps[:, 6, :].rearrange("p (k n) -> p k n", k=KC), ACT.Copy).then_inc(x_parts, 1)

            def expert(e, s, first=False, cols=slice(0, DM), h=0):
                act.wait_ge(t_ready, e + h + 1)
                if not first:
                    act.wait_ge(e_added, e - 1)
                act.activation(re_[:, s, cols], te[:, s, cols], ACT.Relu,
                               scale=wsel[:, bass.ds(e, 1)]).then_inc(r_ready, 1)

            for e in (0, 1):
                expert_high(e + 2, e)
                if e == 0:
                    act.wait_ge(gate_step, 7)
                expert(e, e, first=True)
            with act.Fori(1, NE // 2 - 1) as pair:
                for u in range(2):
                    expert_high(pair * 2 + (u + 2), u)
                    expert(pair * 2 + u, u)
            expert(NE - 2, 0)
            for h in range(2):
                expert(NE - 1, 1, cols=halves[h], h=h)

        @block.vector
        def _(dve):
            def layer_norm(n):
                dve.bn_stats(stats, res[:]).then_inc(ln_step, 1)
                dve.wait_ge(ln_step, n * 4 + 1)
                dve.bn_aggr(mv2, stats).then_inc(ln_step, 1)
                dve.wait_ge(ln_step, n * 4 + 2)
                dve.tensor_scalar(vareps, small[:, 7:8], EPS, None, ALU.add).then_inc(ln_step, 1)
                dve.wait_ge(rstd_ready, n + 1)
                dve.tensor_scalar(xn[:], res[:], mean, rstd, ALU.subtract, ALU.mult).then_inc(ln_step, 1)

            def take_transposed(n, bank):
                dve.wait_ge(xt_psum, n + 1)
                dve.tensor_copy(xT[:], ps[:, bank, :].rearrange("p (k n) -> p k n", k=KC)).then_inc(xt_copied, 1)

            dve.memset(xT[:, 0:2], 0.0).then_inc(warm_set, 1)
            dve.wait_ge(ld_x, 16)
            layer_norm(0)
            dve.wait_ge(ld_cst, 16)
            dve.tensor_copy(identb[:], ident).then_inc(ident_set, 1)
            take_transposed(0, 6)

            def third_part(n):
                dve.wait_ge(part2, n + 1)
                dve.tensor_tensor(parts[:, 2, chunks[n][0]], resid[:, chunks[n][0]], parts[:, 1, chunks[n][0]],
                                  ALU.subtract).then_inc(part3, 1)

            for n in range(5):
                dve.wait_ge(part1, n + 1)
                dve.tensor_tensor(resid[:, chunks[n][0]], ps[:, chunks[n][1], :], parts[:, 0, chunks[n][0]],
                                  ALU.subtract).then_inc(residual, 1)
                third_part(n)

            def maxima(i, first=False):
                for c in range(8):
                    dve.wait_ge(row_scores, i * 8 + c + 1)
                    dve.tensor_reduce(mx[:, c:c + 1], ps[:, 2 * (c % 2):2 * (c % 2) + 2, :],
                                      AX.XY, ALU.max).then_inc(row_maxed, 1)
                dve.wait_ge(row_maxed, i * 8 + 8)
                dve.tensor_reduce(nm, mx.rearrange("p (c r) -> p r c", c=2), AX.X, ALU.max,
                                  negate=True).then_inc(m_step, 1)
                dve.wait_ge(m_step, i * 3 + 1)
                if not first:
                    dve.wait_ge(m_rows, i)
                dve.tensor_copy(mparts[:, :, 0], nm).then_inc(m_step, 1)
                dve.wait_ge(m_step, i * 3 + 2)
                dve.tensor_tensor(mparts[:, :, 1], nm, mparts[:, :, 0], ALU.subtract).then_inc(m_step, 1)

            maxima(0, first=True)
            with dve.Fori(1, KVH) as i:
                maxima(i)

            for f in range(2):
                dve.wait_ge(combined, f + 1)
                dve.tensor_copy(csb[:, f], ps[:, (0, 3)[f], :]).then_inc(comb_copied, 1)
                dve.wait_ge(otr, f + 1)
                by_head = ps[:, 2, :].rearrange("p (r j c) -> p r j c", r=REP, j=4)
                dve.reciprocal(rden[:, 16 * f:16 * f + 16].rearrange("p (n o) -> p n o", o=1),
                               ps[:, 2, :].rearrange("p (n c) -> p n c", c=32)[:, :, HD:HD + 1]
                               ).then_inc(onorm, 1)
                dve.wait_ge(onorm, 2 * f + 1)
                dve.tensor_tensor(
                    otok[:, 256 * f:256 * f + 256].rearrange("p (j r c) -> p r j c", j=4, r=REP),
                    by_head[:, :, :, 0:HD],
                    rden[:, 16 * f:16 * f + 16].rearrange("p (r j) -> p r j", r=REP).unsqueeze(3)
                    .to_broadcast([P, REP, 4, HD]), ALU.mult).then_inc(onorm, 1)
                dve.wait_ge(ot_psum, f + 1)
                dve.tensor_copy(xT[:, 2 * f:2 * f + 2], ps[:, 0, 256 * f:256 * f + 256].rearrange(
                    "p (k n) -> p k n", k=2)).then_inc(ot_copied, 1)
            dve.wait_ge(attn_psum, 1)
            dve.tensor_tensor(res[:], ps[:, 1, :], res[:], ALU.add).then_inc(attn_added, 1)
            dve.wait_ge(attn_added, 1)
            layer_norm(1)
            dve.memset(pre[:, :, 0:TAPS - 1], 0.0)
            take_transposed(1, 6)

            def step(n):
                dve.wait_ge(dt_step, n)

            dve.wait_ge(dt_psum, 1)
            dve.wait_ge(ld_par, 48)
            dve.tensor_tensor(z, ps[:, 7, 0:P], dtb[:], ALU.add).then_inc(dt_step, 1)
            step(1)
            dve.scalar_tensor_tensor(nz, z, -1.0, z, ALU.mult, ALU.min).then_inc(dt_step, 1)
            dve.wait_ge(dt_act, 1)
            dve.tensor_scalar(ez1, ez, 1.0, None, ALU.add).then_inc(dt_step, 1)
            step(3)
            dve.tensor_scalar(dz, ez1, -1.0, 1e-30, ALU.add, ALU.max).then_inc(dt_step, 1)
            step(4)
            dve.reciprocal(rz, dz).then_inc(dt_step, 1)
            step(5)
            dve.tensor_tensor(rz, rz, ez, ALU.mult).then_inc(dt_step, 1)
            step(6)
            dve.wait_ge(dt_act, 2)
            dve.tensor_tensor(rz, rz, lnz, ALU.mult).then_inc(dt_step, 1)
            step(7)
            dve.scalar_tensor_tensor(dt[:], z, 0.0, rz, ALU.max, ALU.add).then_inc(dt_step, 1)
            step(8)
            dve.tensor_scalar(dt[:], dt[:], DT_MIN, DT_MAX, ALU.max, ALU.min).then_inc(dt_step, 1)
            step(9)
            dve.tensor_tensor(dA[:], dt[:], acoef, ALU.mult).then_inc(dt_step, 1)

            def conv(n, h, cp):
                dve.wait_ge(pre_ready, n * 2 + h + 1)
                for k in reversed(range(TAPS - 1)):
                    for j in range(HB):
                        b = HB * h + j
                        if k == TAPS - 2:
                            dve.wait_ge(tap_done, n * 8 + (b + 1))
                        else:
                            dve.wait_ge(conv_step, n * 24 + (12 * h + HB * (TAPS - 3 - k) + j + 1))
                        dve.scalar_tensor_tensor(xs[:, b], pre[:, b, k:k + P], cp[:, b, k:k + 1],
                                                 xs[:, b], ALU.mult, ALU.add).then_inc(conv_step, 1)

            def cs_parts():
                dve.wait_ge(cs_psum, 1)
                dve.tensor_copy(csparts[:, 0], ps[:, 7, P:2 * P]).then_inc(cs_step, 1)
                dve.wait_ge(cs_step, 1)
                dve.tensor_tensor(csres, ps[:, 7, P:2 * P], csparts[:, 0], ALU.subtract).then_inc(cs_step, 1)
                dve.wait_ge(cs_step, 2)
                dve.tensor_copy(csparts[:, 1], csres).then_inc(cs_step, 1)
                dve.wait_ge(cs_step, 3)
                dve.tensor_tensor(csparts[:, 2], csres, csparts[:, 1], ALU.subtract).then_inc(cs_step, 1)

            for h in range(2):
                conv(0, h, par_v[:, 0])
            cs_parts()
            for h in range(2):
                conv(1, h, par_v[:, 1])

            def masked_cb():
                for h in range(2):
                    dve.wait_ge(cb_psum, h + 1)
                    dve.tensor_tensor(cbm[:, 4 * h:4 * h + 4],
                                      ps[:, 6 + h, :].rearrange("p (g n) -> p g n", g=4),
                                      tri.unsqueeze(1).to_broadcast([P, 4, P]), ALU.mult).then_inc(cb_ready, 1)

            def gated(g, first=False):
                dve.wait_ge(xd_ready, g + 1)
                if not first:
                    dve.wait_ge(sq_done, g)
                    dve.wait_ge(yw_ready, g * 2)
                dve.wait_ge(sg_done, g * 2 + 2)
                for h in range(2):
                    at = slice(HB * h, HB * h + HB)
                    dve.wait_ge(y_psum, g * 2 + h + 1)
                    dve.tensor_tensor(yg[:, at], ps[:, 4 + h, :].rearrange("p (b n) -> p b n", b=HB),
                                      xd[:, at], ALU.add).then_inc(u_done, 1)
                    dve.wait_ge(u_done, g * 2 + h + 1)
                    dve.tensor_tensor(yg[:, at], yg[:, at], sg[:, at], ALU.mult).then_inc(yg_ready, 1)

            def sum_squares(g, first=False):
                dve.wait_ge(sq_done, g + 1)
                if not first:
                    dve.wait_ge(ss_psum, g)
                dve.tensor_reduce(sqs[:], xd.rearrange("p b n -> p n b"), AX.X, ALU.add).then_inc(sqs_ready, 1)

            def operand_low(g):
                for h in range(2):
                    dve.wait_ge(ywh_ready, g * 2 + h + 1)
                    dve.tensor_tensor(yw_l[:, HB * h:HB * h + HB], yw[:, HB * h:HB * h + HB],
                                      yw_h[:, HB * h:HB * h + HB], ALU.subtract).then_inc(ywl_ready, 1)

            def weights_low(g, q):
                dve.wait_ge(woh_ready, g * 4 + 4)
                at = slice(2 * q, 2 * q + 2)
                dve.tensor_tensor(wo_l[:, at], wo_v[:, at], wo_h[:, at], ALU.subtract).then_inc(wol3_ready, 1)

            def group_variance(g):
                dve.wait_ge(ss_psum, g + 1)
                dve.tensor_scalar(gvar, ps[:, 7, 0:1], 1.0 / GROUP, EPS, ALU.mult, ALU.add).then_inc(gvar_ready, 1)

            def add_group(g):
                dve.wait_ge(grstd_ready, g + 1)
                dve.wait_ge(o_psum, g + 1)
                dve.scalar_tensor_tensor(res[:], ps[:, 6, :], grstd, res[:], ALU.mult, ALU.add).then_inc(o_added, 1)

            def times_dt(g):
                for h in range(2):
                    dve.wait_ge(xtok_psum, g * 2 + h + 1)
                    dve.tensor_tensor(
                        xdt[:, GB * h:GB * h + GB], ps[:, h, :].rearrange("p (n c) -> p n c", n=8),
                        dt[:, bass.ds(g * GH + GB * h, GB)].unsqueeze(2).to_broadcast([P, GB, 64]),
                        ALU.mult).then_inc(xdt_ready, 1)

            def group(g, first=False, second=False):
                if not first:
                    gated(g - 1, first=second)
                    weights_low(g - 1, 3)
                    operand_low(g - 1)
                    sum_squares(g - 1, first=second)
                if first:
                    conv(2, 0, par_v[:, 2])
                    masked_cb()
                    conv(2, 1, par_v[:, 2])
                    dve.wait_ge(cb_ready, 2)
                else:
                    for h in range(2):
                        conv(g + 2, h, cpar)
                    group_variance(g - 1)
                if first:
                    times_dt(g)
                for c in range(4):
                    dve.wait_ge(decay_done, g * 4 + c + 1)
                    dve.tensor_tensor(em[:, c], em[:, c], cbm[:, bass.ds(g, 1)].to_broadcast([P, 4, P]),
                                      ALU.mult).then_inc(em_ready, 1)
                if not first:
                    add_group(g - 1)
                    times_dt(g)

            group(0, first=True)
            group(1, second=True)
            with dve.Fori(2, NG) as g:
                group(g)
            gated(NG - 1)
            weights_low(NG - 1, 3)
            operand_low(NG - 1)
            sum_squares(NG - 1)
            weights_low(NG - 1, 2)

            def expert_low(e, s):
                dve.wait_ge(weh_ready, e * 2 + 2)
                dve.tensor_tensor(we_l[:, bass.ds(e, 1), 2:4].rearrange("p o k n -> p (o k) n"),
                                  we[:, bass.ds(e, 1), 2:4].rearrange("p o k n -> p (o k) n"),
                                  we_h[:, s, 2:4], ALU.subtract).then_inc(wel_dve, 1)

            group_variance(NG - 1)
            expert_low(0, 0)
            add_group(NG - 1)
            dve.wait_ge(o_added, NG)
            layer_norm(2)
            expert_low(1, 1)
            dve.wait_ge(x_parts, 1)
            take_transposed(2, 6)
            dve.wait_ge(xt_copied, 3)
            dve.tensor_tensor(x_l, xT[:], x_h, ALU.subtract).then_inc(x_parts, 1)
            dve.wait_ge(lg_psum, 1)
            dve.tensor_tensor(lg, ps[:, 7, 0:NE], bgate[:], ALU.add).then_inc(gate_step, 1)
            dve.wait_ge(gate_step, 1)
            lg_j = lg.unsqueeze(1).to_broadcast([P, NE, NE])
            lg_e = lg.unsqueeze(2).to_broadcast([P, NE, NE])
            dve.tensor_tensor(cmp1, lg_j, lg_e, ALU.is_gt).then_inc(gate_step, 1)
            dve.tensor_tensor(cmp2, lg_j, lg_e, ALU.is_equal).then_inc(gate_step, 1)
            dve.wait_ge(gate_step, 3)
            dve.tensor_tensor(cmp2, cmp2, lower, ALU.mult).then_inc(gate_step, 1)
            dve.wait_ge(gate_step, 4)
            dve.tensor_tensor(cmp1, cmp1, cmp2, ALU.add).then_inc(gate_step, 1)
            dve.wait_ge(gate_step, 5)
            dve.tensor_reduce(rank, cmp1, AX.X, ALU.add).then_inc(gate_step, 1)
            dve.wait_ge(gate_step, 6)
            dve.tensor_scalar(wsel, rank, 1.5, 0.5, ALU.is_lt, ALU.mult).then_inc(gate_step, 1)

            def add_bias(e, s, first=False, cols=slice(0, DM), h=0):
                dve.wait_ge(e_psum, e + h + 1)
                if not first:
                    dve.wait_ge(r_ready, e - 1)
                dve.tensor_tensor(te[:, s, cols], ps[:, s + h, cols],
                                  be[:, bass.ds(e, 1), cols].rearrange("p o n -> p (o n)"),
                                  ALU.add).then_inc(t_ready, 1)

            def add_expert(e, s, first=False, cols=slice(0, DM), h=0):
                dve.wait_ge(r_ready, e + h + 1)
                if not first:
                    dve.wait_ge(e_added, e)
                dve.tensor_tensor(res[:, cols], res[:, cols], re_[:, s, cols], ALU.add).then_inc(e_added, 1)

            dve.wait_ge(ld_be, 16)
            add_bias(0, 0, first=True)
            expert_low(2, 0)
            add_bias(1, 1, first=True)
            expert_low(3, 1)
            add_expert(0, 0, first=True)
            with dve.Fori(1, NE // 2 - 1) as pair:
                for u in range(2):
                    add_bias(pair * 2 + u, u)
                    expert_low(pair * 2 + (u + 2), u)
                    add_expert(pair * 2 + u - 1, 1 - u)
            add_bias(NE - 2, 0)
            add_expert(NE - 3, 1)
            add_bias(NE - 1, 1, cols=halves[0])
            add_expert(NE - 2, 0)
            add_bias(NE - 1, 1, cols=halves[1], h=1)
            for h in range(2):
                add_expert(NE - 1, 1, cols=halves[h], h=h)

        @block.tensor
        def _(pe):
            def keep_warm(n, bank):
                for _ in range(n):
                    pe.matmul(ps[:, bank, :], identb[:], csr[:, 0:512], start=True, stop=True)

            def transpose_xn(n, src, bank):
                for k in range(KC):
                    last = pe.transpose(ps[:, bank, P * k:P * k + P], src[:, P * k:P * k + P], ident)
                last.then_inc(xt_psum, 1)

            def project_k(t, ks=range(KC)):
                if t:
                    pe.wait_ge(ld_ctx[t], 16)
                for k in ks:
                    if t == 0 and k % 2 == 0:
                        pe.wait_ge(ld_ctx0[k // 2], 16)
                    last = pe.matmul(ps[:, t, :], wk[:, k], ctxT[:, t, k], start=k == 0, stop=k == KC - 1)
                if ks[-1] == KC - 1:
                    last.then_inc(qk_psum, 1)

            pe.wait_ge(warm_set, 1)
            for n in range(WARM):
                pe.matmul(ps[:, 6, :], warm[:, 0:P], warm[:, 0:512], start=True, stop=True)
            pe.wait_ge(ld_wk, 16)
            project_k(0)
            project_k(1, range(0, 2))
            pe.wait_ge(ld_cst, 16)
            pe.wait_ge(ln_step, 4)
            transpose_xn(0, xn, 6)
            project_k(1, range(2, KC))
            pe.wait_ge(xt_copied, 1)
            pe.wait_ge(ld_wq, 16)
            for r in range(REP):
                for k in range(KC):
                    last = pe.matmul(ps[:, 7, P * r:P * r + P], wq[:, k, P * r:P * r + P], xT[:, k],
                                     start=k == 0, stop=k == KC - 1)
            last.then_inc(qk_psum, 1)
            for t in range(QN, 4):
                project_k(t)
            pe.wait_ge(ld_wv, 16)

            def project_v(t, b):
                if b == 0 and t >= 2:
                    pe.wait_ge(v_copied, t - 1)
                for k in range(KC):
                    last = pe.matmul(ps[:, 4 + t % 2, P * b:P * b + P], ctxT[:, t, k, P * b:P * b + P],
                                     wv[:, k], start=k == 0, stop=k == KC - 1)
                if b == 3:
                    last.then_inc(v_psum, 1)

            def rows(i, s, c, first=False):
                if not first:
                    pe.wait_ge(row_maxed, i * 8 + c - 1)
                r, half = c % REP, c // REP
                for j in range(2):
                    at = 1024 * half + 512 * j
                    last = pe.matmul(ps[:, 2 * (c % 2) + j, :], kq[0:KROWS, s, KCOLS + P * r:KCOLS + P * r + P],
                                     kq[0:KROWS, s, at:at + 512], start=True, stop=True)
                last.then_inc(row_scores, 1)

            def maxima_to_rows(i, s):
                pe.wait_ge(m_step, i * 3 + 3)
                bank = score_bank(s, NKB)
                for r in range(REP):
                    last = pe.matmul(ps[KROWS:KROWS + MROWS, bank, P * r:P * r + P], mparts[:, r], identb[:],
                                     start=True, stop=True, tile_position=(0, KROWS))
                last.then_inc(m_rows, 1)

            def columns(i, s, b, first=False):
                if b == 0:
                    pe.wait_ge(m_copied, i + 1)
                if b > 2:
                    pe.wait_ge(probs, i * NKB + (b - 2))
                elif b < 2 and not first:
                    pe.wait_ge(probs, i * NKB + (b - 1))
                pe.matmul(ps[:, score_bank(s, b), :], kq[0:KROWS + MROWS, s, P * b:P * b + P],
                          kq[0:KROWS + MROWS, s, KCOLS:], start=True, stop=True).then_inc(scores, 1)

            def product(i, s, grp):
                pe.wait_ge(probs, i * NKB + 4 * grp + 4)
                if grp == 0:
                    pe.wait_ge(vslot_ready, i + 1)
                for j in range(4):
                    last = pe.matmul(ps[32 * j:32 * j + 32, 6, :], vw[:, s, 4 * grp + j], pb[:, (4 * grp + j) % 8],
                                     start=grp == 0, stop=grp == 3, tile_position=(0, 32 * j))
                last.then_inc(pv_groups, 1)

            def quarter(i, s, grp, turns=None, ahead=True, maxima=True):
                n, c = (i + 1, 2 * grp + 2) if grp < 3 else (i + 2, 0)
                slot = (s + (1 if grp < 3 else 2)) % SLOTS
                first = isinstance(i, int) and i == 0
                columns(i, s, 4 * grp, first)
                columns(i, s, 4 * grp + 1, first)
                if ahead:
                    if grp == 3:
                        pe.wait_ge(ld_kq[slot], turns)
                    rows(n, slot, c)
                if grp in (1, 2):
                    product(i, s, grp - 1)
                elif grp == 0 and not first:
                    product(i - 1, (s + 2) % SLOTS, 3)
                columns(i, s, 4 * grp + 2, first)
                if ahead and grp < 3:
                    rows(n, slot, c + 1)
                columns(i, s, 4 * grp + 3, first)
                if grp == 3 and maxima:
                    pe.wait_ge(probs, i * NKB + 14)
                    maxima_to_rows(i + 1, s)
                if grp == 3:
                    product(i, s, 2)
                if ahead and grp == 3:
                    rows(n, slot, c + 1)

            pe.wait_ge(const_set, 6)
            n_v = 0
            for c in range(8):
                while n_v < (3 + c if c < 4 else 4 + c):
                    project_v(n_v // 4, n_v % 4)
                    n_v += 1
                if c == 0:
                    pe.wait_ge(ld_kq_early, KQ_EARLY)
                    pe.wait_ge(residual, 5)
                if c == 4:
                    pe.wait_ge(ld_kq[0], KQ_REST)
                rows(0, 0, c, first=c < 2)
            for n in range(n_v, NKB):
                project_v(n // 4, n % 4)
            pe.wait_ge(ld_kq[1], KQ_LOADS)
            rows(1, 1, 0)
            rows(1, 1, 1)
            pe.wait_ge(ident_set, 1)
            pe.wait_ge(v_copied, 4)
            maxima_to_rows(0, SLOTS - 1)
            quarter(0, 0, 0)
            with pe.Fori(0, 2) as t:
                for u in range(3):
                    turns = t * KQ_LOADS + (KQ_LOADS * ((u + 2) // SLOTS + 1)
                                            - (KQ_LOADS - KQ_REST) * ((u + 2) % SLOTS == 0))
                    for grp in range(1, 4):
                        quarter(t * 3 + u, u, grp, turns)
                    quarter(t * 3 + (u + 1), (u + 1) % SLOTS, 0)
            for grp in range(1, 4):
                quarter(KVH - 2, (KVH - 2) % SLOTS, grp, ahead=grp < 3)

            def combine(f, js):
                pe.wait_ge(pv_saved, 4 * f + js[-1] + 1)
                for j in js:
                    last = pe.matmul(ps[32 * j:32 * j + 32, (0, 3)[f], :], comb, pvs[:, 4 * f + j],
                                     start=True, stop=True, tile_position=(0, 32 * j))
                if js[-1] == 3:
                    last.then_inc(combined, 1)

            def by_token(f):
                pe.wait_ge(comb_copied, f + 1)
                if f:
                    pe.wait_ge(onorm, 2)
                for r in range(REP):
                    last = pe.transpose(ps[:, 2, P * r:P * r + P], csb[:, f, P * r:P * r + P], ident)
                last.then_inc(otr, 1)

            def by_feature(f):
                pe.wait_ge(onorm, 2 * f + 2)
                for k in (2 * f, 2 * f + 1):
                    last = pe.transpose(ps[:, 0, P * k:P * k + P], otok[:, P * k:P * k + P], ident)
                last.then_inc(ot_psum, 1)

            def project_attention(f):
                pe.wait_ge(ot_copied, f + 1)
                for k in (2 * f, 2 * f + 1):
                    last = pe.matmul(ps[:, 1, :], xT[:, k], woa[:, k], start=k == 0, stop=k == KC - 1)
                if f:
                    last.then_inc(attn_psum, 1)

            i, s = KVH - 1, (KVH - 1) % SLOTS
            pe.wait_ge(row_maxed, 8 * KVH)
            quarter(i, s, 0, ahead=False)
            combine(0, (0, 1, 2, 3))
            quarter(i, s, 1, ahead=False)
            combine(1, (0, 1, 2))
            by_token(0)
            quarter(i, s, 2, ahead=False)
            by_feature(0)
            quarter(i, s, 3, ahead=False, maxima=False)
            product(i, s, 3)
            pe.wait_ge(ld_woa, 16)
            project_attention(0)
            combine(1, (3,))
            by_token(1)
            by_feature(1)
            project_attention(1)

            pe.wait_ge(ld_csconst, 32)
            keep_warm(14, 5)
            pe.wait_ge(ln_step, 8)
            transpose_xn(1, xn, 6)
            keep_warm(4, 5)
            pe.wait_ge(xt_copied, 2)
            pe.wait_ge(ld_wdt, 32)
            for k in range(KC):
                last = pe.matmul(ps[:, 7, 0:P], xT[:, k], wdt[:, k], start=k == 0, stop=k == KC - 1)
            last.then_inc(dt_psum, 1)

            def project(w, banks, done, halves=(0, 1)):
                for b in range(HB * halves[0], HB * halves[-1] + HB):
                    for k in range(KC):
                        last = pe.matmul(ps[:, banks + b // HB, P * (b % HB):P * (b % HB) + P],
                                         w[:, b, k], xT[:, k], start=k == 0, stop=k == KC - 1)
                    if b % HB == HB - 1:
                        last.then_inc(done, 1)

            pe.wait_ge(ld_wg, 16)
            project(wg, 0, proj_psum)
            pe.wait_ge(dt_step, 10)
            pe.matmul(ps[:, 7, P:2 * P], dA[:], tri, start=True, stop=True).then_inc(cs_psum, 1)
            pe.wait_ge(ld_wo, 16)
            project(wc_v, 2, proj_psum)

            def out_proj(g, first=False, between=None, last_group=False):
                if not first:
                    pe.wait_ge(o_added, g)
                for n in range(3):
                    if n == 2 and between is not None:
                        segments(between, (2, 3))
                    if n == (2 if last_group else 1):
                        pe.wait_ge(sqs_ready, g + 1)
                        pe.matmul(ps[:, 7, 0:1], sqs[:], ones1, start=True, stop=True).then_inc(ss_psum, 1)
                    for b in range(GB):
                        if n < 2 and b % HB == 0:
                            pe.wait_ge((ywh_ready, ywl_ready)[n], g * 2 + b // HB + 1)
                        if n == 0 and b % 2 == 0:
                            pe.wait_ge(woh_ready, g * 4 + b // 2 + 1)
                        if n == 2 and b == 6:
                            pe.wait_ge(wol3_ready, g + 1)
                        elif n == 2 and b == 4 and last_group:
                            pe.wait_ge(wol3_ready, g + 2)
                        elif n == 2 and b % 2 == 0:
                            pe.wait_ge(wol_ready, g * 3 + b // 2 + 1)
                        last = pe.matmul(ps[:, 6, :], (yw_l if n == 1 else yw_h)[:, b],
                                         (wo_l if n == 2 else wo_h)[:, b],
                                         start=n == 0 and b == 0, stop=n == 2 and b == GB - 1)
                last.then_inc(o_psum, 1)

            def segments(g, cs):
                for c in cs:
                    if c >= 2:
                        pe.wait_ge(clamped, g * 4 + c - 1)
                    pe.matmul(ps[:, 4 + c % 2, :], csl[:], csr[:, 512 * c:512 * c + 512],
                              start=True, stop=True).then_inc(seg_psum, 1)

            def gates(g, first=False, halves=(0, 1)):
                pe.wait_ge(ld_wg, g * 16 + 32)
                if first:
                    pe.wait_ge(tap_done, 16)
                else:
                    pe.wait_ge(sg_done, g * 2)
                project(wg, 2, gate_psum, halves)

            def group(g, first=False, second=False):
                pe.wait_ge(ld_wx, g * 16 + 16)
                if first:
                    pe.wait_ge(tap_done, 8)
                else:
                    pe.wait_ge(xdt_ready, g * 2)
                project(wx, 0, proj_psum)
                if first:
                    pe.wait_ge(ld_cs, 32)
                    segments(g, (0, 1))
                    pe.wait_ge(silu_done, 4)
                    for n in range(NG):
                        last = pe.matmul(ps[:, 6 + n // 4, P * (n % 4):P * (n % 4) + P], bt[:, n], ct[:, n],
                                         start=True, stop=True)
                        if n % 4 == 3:
                            last.then_inc(cb_psum, 1)
                    segments(g, (2, 3))
                    gates(g, first=True, halves=(0,))
                else:
                    pe.wait_ge(u_done, g * 2)
                    pe.wait_ge(ld_cs, g * 32 + 32)
                    segments(g, (0, 1))
                    out_proj(g - 1, first=second, between=g)
                for h in range(2):
                    pe.wait_ge(silu_done, g * 2 + h + 5)
                    for b in range(HB):
                        last = pe.transpose(ps[:, h, P * b:P * b + P], xs[:, HB * h + b], ident)
                    last.then_inc(xtok_psum, 1)
                    if not first:
                        gates(g, halves=(h,))
                if first:
                    gates(g, first=True, halves=(1,))
                pe.wait_ge(em_ready, g * 4 + 4)
                pe.wait_ge(xdt_ready, g * 2 + 2)
                for b in range(GB):
                    for o in range(2):
                        h = 2 * b + o
                        last = pe.matmul(ps[64 * o:64 * o + 64, 4 + b // HB, P * (b % HB):P * (b % HB) + P],
                                         xdt[:, h], em[:, h // 4, h % 4], start=True, stop=True,
                                         tile_position=(0, 64 * o))
                    if b % HB == HB - 1:
                        last.then_inc(y_psum, 1)

            group(0, first=True)
            group(1, second=True)
            with pe.Fori(2, NG) as g:
                group(g)
            keep_warm(13, 0)
            out_proj(NG - 1, last_group=True)

            keep_warm(14, 2)
            pe.wait_ge(ln_step, 12)
            transpose_xn(2, xn, 6)
            keep_warm(4, 2)

            def expert(e, bank, s, first=False, cols=slice(0, DM)):
                if not first:
                    pe.wait_ge(t_ready, e - 1)
                for n in range(3):
                    for k in range(KC):
                        if n == 0 and k % 2 == 0:
                            pe.wait_ge(weh_ready, e * 2 + (k // 2 + 1))
                        if n == 2 and k % 2 == 0:
                            pe.wait_ge((wel_pool, wel_dve)[k // 2], e + 1)
                        w = we_h[:, s, k, cols]
                        if n == 2:
                            w = we_l[:, bass.ds(e, 1), k, cols].rearrange("p o n -> p (o n)")
                        if first and e == 0 and k == 0 and n < 2:
                            pe.wait_ge(x_parts, n + 1)
                        last = pe.matmul(ps[:, bank, cols], (x_l if n == 1 else x_h)[:, k], w,
                                         start=n == 0 and k == 0, stop=n == 2 and k == KC - 1)
                last.then_inc(e_psum, 1)

            expert(0, 0, 0, first=True)
            pe.wait_ge(xt_copied, 3)
            for k in range(KC):
                last = pe.matmul(ps[:, 7, 0:NE], xT[:, k], wgate[:, k], start=k == 0, stop=k == KC - 1)
            last.then_inc(lg_psum, 1)
            expert(1, 1, 1, first=True)
            with pe.Fori(1, NE // 2 - 1) as pair:
                for u in range(2):
                    expert(pair * 2 + u, u, u)
            expert(NE - 2, 0, 0)
            for h in range(2):
                expert(NE - 1, 1 + h, 1, cols=halves[h])


def kernel(x, ctx_4096, L0_xattn_Wq, L0_xattn_Wk, L0_xattn_Wv, L0_xattn_Wo, L0_attn_in_proj_w,
           L0_attn_conv_w, L0_attn_conv_b, L0_attn_dt_bias, L0_attn_D, L0_attn_norm_w,
           L0_attn_out_proj_w, L0_ffn_W_gate, L0_ffn_b_gate, L0_ffn_W_e, L0_ffn_b_e):
    import numpy as np
    from ml_dtypes import bfloat16 as bf16
    import concourse.bacc as bacc
    from concourse.bass_utils import run_bass_kernel_spmd

    f = np.float32
    inter = NG * GROUP
    a = {}

    def by_partition(w):
        return w.reshape(KC, P, w.shape[-1]).transpose(1, 0, 2)

    i = np.arange(P)
    cst = np.zeros((P, C_END), f)
    cst[:, C_ID:C_ID + P] = np.eye(P)
    cst[:, C_TRI:C_TRI + P] = i[:, None] <= i[None, :]
    cst[:, C_A:C_A + P] = -(i[None, :] + 1.0)
    cst[:, C_COMB:C_COMB + HD] = (i % 32)[:, None] == np.arange(HD)[None, :]
    cst[:, C_COMB + HD:C_COMB + 32] = ((i % 32) == HD)[:, None]
    cst[:, C_LT:C_END] = np.tril(np.ones((NE, NE)), -1).ravel()[None, :]
    a["cst"] = cst

    csl = np.zeros((P, P), bf16)
    csl[:CPARTS] = 1
    csr = np.zeros((P, GH, P), bf16)
    for h in range(GH):
        csr[CPARTS * (h + 1):CPARTS * (h + 2), h] = -1
    a["csl"], a["csr"] = csl, csr.reshape(P, GH * P)

    a["x"] = np.asarray(x).reshape(P, DM)
    a["ctx"] = np.asarray(ctx_4096).reshape(4, 512, KC, P).transpose(0, 3, 2, 1)
    wq = np.asarray(L0_xattn_Wq).reshape(DM, KVH, REP, HD).transpose(0, 2, 1, 3).reshape(DM, DM)
    a["wq"] = by_partition(wq)
    a["wk"] = by_partition(np.asarray(L0_xattn_Wk))
    a["wv"] = by_partition(np.asarray(L0_xattn_Wv))
    a["woa"] = by_partition(np.asarray(L0_xattn_Wo))
    w = np.asarray(L0_attn_in_proj_w)

    def blocks(rows):
        return rows.reshape(-1, GB, P, KC, P).transpose(0, 4, 1, 3, 2)

    a["wg"] = blocks(w[:inter])
    a["wx"] = blocks(w[inter:2 * inter])
    a["wbc"] = blocks(w[2 * inter:2 * inter + 2 * NG * P])
    a["wdt"] = by_partition(w[2 * inter + 2 * NG * P:].T)
    a["wout"] = np.asarray(L0_attn_out_proj_w).reshape(DM, NG, GB, P).transpose(1, 3, 2, 0)
    cols = np.zeros((P, NG + 2, GB, NPAR), f)
    order = list(range(NG, NG + 2)) + list(range(NG))
    cols[..., 0:TAPS] = np.asarray(L0_attn_conv_w).reshape(NG + 2, GB, P, TAPS).transpose(2, 0, 1, 3)[:, order]
    cols[..., 4] = np.asarray(L0_attn_conv_b).reshape(NG + 2, GB, P).transpose(2, 0, 1)[:, order]
    cols[:, 2:, :, 5] = np.repeat(np.asarray(L0_attn_D), 64).reshape(NG, GB, P).transpose(2, 0, 1)
    cols[:, 2:, :, 6] = np.asarray(L0_attn_norm_w).reshape(NG, GB, P).transpose(2, 0, 1)
    a["par"] = cols.reshape(P, NG + 2, GB * NPAR)
    a["dtb"] = np.asarray(L0_attn_dt_bias).reshape(1, P)
    a["bgate"] = np.asarray(L0_ffn_b_gate).reshape(1, NE)
    a["wgate"] = by_partition(np.asarray(L0_ffn_W_gate))
    a["we"] = np.asarray(L0_ffn_W_e).reshape(NE, KC, P, DM).transpose(0, 2, 1, 3)
    a["be"] = np.asarray(L0_ffn_b_e).reshape(1, NE * DM)

    nc = bacc.Bacc("TRN2", target_bir_lowering=False, num_devices=1)
    arrays, d = {}, {}
    for name, v in a.items():
        v = np.ascontiguousarray(v)
        arrays[f"in_{name}"] = v
        d[name] = nc.dram_tensor(f"in_{name}", v.shape, mybir.dt.from_np(v.dtype), kind="ExternalInput").ap()
    d["cs"] = nc.dram_tensor("cs_parts", (P, CPARTS, P), BF16).ap()
    d["out"] = nc.dram_tensor("out", (1, P, DM), F32, kind="ExternalOutput").ap().rearrange("a b c -> (a b) c")
    build(nc, d)
    r = run_bass_kernel_spmd(nc, [arrays], core_ids=[0])
    return r.results[0]["out"]
```
